# Optimizing a Trainium2 kernel written in Bass

```python
import numpy as np
import jax
import jax.numpy as jnp

def _softmax(x, axis=-1):
    return jax.nn.softmax(x, axis=axis)

def _gelu(x):
    return jax.nn.gelu(x, approximate=True)

def _silu(x):
    return jax.nn.silu(x)

def _sigmoid(x):
    return jax.nn.sigmoid(x)

def _layernorm(x, axis=-1, eps=1e-05):
    m = jnp.mean(x, axis=axis, keepdims=True)
    v = jnp.var(x, axis=axis, keepdims=True)
    return (x - m) / jnp.sqrt(v + eps)

def _scatter_add(tgt, idx, src, axis=0):
    return tgt.at[idx].add(src)

def _segment_sum(src, seg, n):
    return jax.ops.segment_sum(src, seg, n)
kernel_name = 'mk_metaformer_d1_conv_nhwc256_r4_6ef7ac'

def setup_inputs(seed: int=0):
    np.random.seed(seed)
    _w = jnp.asarray

    def _rec_inputs():
        import jax
        import jax.numpy as jnp
        _gk = jax.random.key(seed)
        x = -9.26e-05 + 0.9999 * jax.random.normal(jax.random.fold_in(_gk, 1), (4, 48, 48, 64), jnp.float32)
        return x
    x = _rec_inputs()

    def _L0_conv_setup():
        import jax, jax.numpy as jnp
        import numpy as np
        DIM = 64
        HEADS = 8
        HD = DIM // HEADS
        WS = (8, 8)
        DS = (2, 2)
        SH = (4, 4)
        TW = (WS[0] * DS[0], WS[1] * DS[1])
        SCALE = HD ** (-0.5)
        N = WS[0] * WS[1]

        def _rope2(t):
            G, wh, ww, hd = t.shape
            da = hd // 2
            half = da // 2
            inv = 1.0 / 10000.0 ** (jnp.arange(half, dtype=jnp.float32) / half)

            def cs(n):
                ang = jnp.arange(n, dtype=jnp.float32)[:, None] * inv
                return (jnp.cos(ang), jnp.sin(ang))
            cH, sH = cs(wh)
            cW, sW = cs(ww)

            def rot(u, c, s):
                u1, u2 = (u[..., :half], u[..., half:])
                return jnp.concatenate([u1 * c - u2 * s, u1 * s + u2 * c], axis=-1)
            th = rot(t[..., :da], cH[None, :, None, :], sH[None, :, None, :])
            tw = rot(t[..., da:], cW[None, None, :, :], sW[None, None, :, :])
            return jnp.concatenate([th, tw], axis=-1)

        def _build_mask(H, W):
            img = np.zeros((H, W), dtype=np.float32)
            h_sl = (slice(0, -WS[0]), slice(-WS[0], -SH[0]), slice(-SH[0], None))
            w_sl = (slice(0, -WS[1]), slice(-WS[1], 0), slice(0, None))
            cnt = 0
            for hs in h_sl:
                for wsl in w_sl:
                    img[hs, wsl] = cnt
                    cnt += 1
            nH, nW = (H // TW[0], W // TW[1])
            mw = img.reshape(nH, TW[0], nW, TW[1]).transpose(0, 2, 1, 3).reshape(-1, TW[0], TW[1])
            Bm = mw.shape[0]
            mw = mw.reshape(Bm, WS[0], DS[0], WS[1], DS[1]).transpose(0, 1, 3, 2, 4).reshape(Bm, N, DS[0] * DS[1]).transpose(0, 2, 1).reshape(Bm * DS[0] * DS[1], N)
            am = np.where(mw[:, None, :] != mw[:, :, None], -np.inf, 0.0).astype(np.float32)
            return jnp.asarray(am)
        key = jax.random.key(seed)
        k1, k2, k3 = jax.random.split(key, 3)
        x = jax.random.normal(k1, (4, 48, 48, DIM), dtype=jnp.float32)
        W_qkv = jax.random.normal(k2, (DIM, 3 * DIM), dtype=jnp.float32) * 0.02
        b_qkv = jnp.zeros((3 * DIM,), dtype=jnp.float32)
        W_proj = jax.random.normal(k3, (DIM, DIM), dtype=jnp.float32) * 0.02
        b_proj = jnp.zeros((DIM,), dtype=jnp.float32)
        return {'x': x, 'W_qkv': W_qkv, 'b_qkv': b_qkv, 'W_proj': W_proj, 'b_proj': b_proj}
    _L0_conv_all = _L0_conv_setup()
    _L0_conv_in = {k: v for k, v in _L0_conv_all.items() if k in ('W_qkv', 'b_qkv', 'W_proj', 'b_proj')}
    del _L0_conv_all

    def _L0_ffn_setup():
        import jax, jax.numpy as jnp
        import numpy as np
        N_EXPERTS = 8
        TOP_K = 2
        key = jax.random.key(seed)
        ks = jax.random.split(key, 5)
        B, T, C, E, H = (8, 512, 64, 8, 682)
        scale = 1.0 / np.sqrt(C)
        return {'x': jax.random.normal(ks[0], (B, T, C), dtype=jnp.float32), 'router_w': jax.random.normal(ks[1], (E, C), dtype=jnp.float32) * scale, 'w1': jax.random.normal(ks[2], (E, H, C), dtype=jnp.float32) * scale, 'w2': jax.random.normal(ks[3], (E, C, H), dtype=jnp.float32) * (1.0 / np.sqrt(H)), 'w3': jax.random.normal(ks[4], (E, H, C), dtype=jnp.float32) * scale}
    _L0_ffn_all = _L0_ffn_setup()
    _L0_ffn_in = {k: v for k, v in _L0_ffn_all.items() if k in ('router_w', 'w1', 'w2', 'w3')}
    del _L0_ffn_all
    return {'x': x, 'L0_conv_W_qkv': _L0_conv_in['W_qkv'], 'L0_conv_b_qkv': _L0_conv_in['b_qkv'], 'L0_conv_W_proj': _L0_conv_in['W_proj'], 'L0_conv_b_proj': _L0_conv_in['b_proj'], 'L0_ffn_router_w': _L0_ffn_in['router_w'], 'L0_ffn_w1': _L0_ffn_in['w1'], 'L0_ffn_w2': _L0_ffn_in['w2'], 'L0_ffn_w3': _L0_ffn_in['w3']}

def reference(x, L0_conv_W_qkv, L0_conv_b_qkv, L0_conv_W_proj, L0_conv_b_proj, L0_ffn_router_w, L0_ffn_w1, L0_ffn_w2, L0_ffn_w3):
    import jax
    import jax.numpy as jnp

    def _L0_conv_ref(x, W_qkv, b_qkv, W_proj, b_proj):
        import jax, jax.numpy as jnp
        import numpy as np
        DIM = 64
        HEADS = 8
        HD = DIM // HEADS
        WS = (8, 8)
        DS = (2, 2)
        SH = (4, 4)
        TW = (WS[0] * DS[0], WS[1] * DS[1])
        SCALE = HD ** (-0.5)
        N = WS[0] * WS[1]

        def _rope2(t):
            G, wh, ww, hd = t.shape
            da = hd // 2
            half = da // 2
            inv = 1.0 / 10000.0 ** (jnp.arange(half, dtype=jnp.float32) / half)

            def cs(n):
                ang = jnp.arange(n, dtype=jnp.float32)[:, None] * inv
                return (jnp.cos(ang), jnp.sin(ang))
            cH, sH = cs(wh)
            cW, sW = cs(ww)

            def rot(u, c, s):
                u1, u2 = (u[..., :half], u[..., half:])
                return jnp.concatenate([u1 * c - u2 * s, u1 * s + u2 * c], axis=-1)
            th = rot(t[..., :da], cH[None, :, None, :], sH[None, :, None, :])
            tw = rot(t[..., da:], cW[None, None, :, :], sW[None, None, :, :])
            return jnp.concatenate([th, tw], axis=-1)

        def _build_mask(H, W):
            img = np.zeros((H, W), dtype=np.float32)
            h_sl = (slice(0, -WS[0]), slice(-WS[0], -SH[0]), slice(-SH[0], None))
            w_sl = (slice(0, -WS[1]), slice(-WS[1], 0), slice(0, None))
            cnt = 0
            for hs in h_sl:
                for wsl in w_sl:
                    img[hs, wsl] = cnt
                    cnt += 1
            nH, nW = (H // TW[0], W // TW[1])
            mw = img.reshape(nH, TW[0], nW, TW[1]).transpose(0, 2, 1, 3).reshape(-1, TW[0], TW[1])
            Bm = mw.shape[0]
            mw = mw.reshape(Bm, WS[0], DS[0], WS[1], DS[1]).transpose(0, 1, 3, 2, 4).reshape(Bm, N, DS[0] * DS[1]).transpose(0, 2, 1).reshape(Bm * DS[0] * DS[1], N)
            am = np.where(mw[:, None, :] != mw[:, :, None], -np.inf, 0.0).astype(np.float32)
            return jnp.asarray(am)
        Bs, H, W, C = x.shape
        nH, nW = (H // TW[0], W // TW[1])
        nWm = nH * nW * DS[0] * DS[1]
        B_ = Bs * nWm
        Bwin = Bs * nH * nW
        mask = _build_mask(H, W)
        qkv = x.reshape(Bs * H * W, C) @ W_qkv + b_qkv
        qkv = qkv.reshape(B_, N, 3, HEADS, HD).transpose(2, 0, 3, 1, 4)
        q, k, v = (qkv[0], qkv[1], qkv[2])
        q = _rope2(q.reshape(-1, WS[0], WS[1], HD)).reshape(B_, HEADS, N, HD)
        k = _rope2(k.reshape(-1, WS[0], WS[1], HD)).reshape(B_, HEADS, N, HD)
        attn = jnp.einsum('bhnd,bhmd->bhnm', q * SCALE, k)
        attn = attn.reshape(Bs, nWm, HEADS, N, N) + mask[None, :, None, :, :]
        attn = jax.nn.softmax(attn, axis=-1).reshape(B_, HEADS, N, N)
        out = jnp.einsum('bhnm,bhmd->bhnd', attn, v)
        out = out.transpose(0, 2, 1, 3).reshape(B_, N, C)
        out = out.reshape(Bwin, DS[0] * DS[1], N, C).transpose(0, 2, 1, 3)
        out = out.reshape(Bwin, WS[0], WS[1], DS[0], DS[1], C).transpose(0, 1, 3, 2, 4, 5).reshape(Bwin, TW[0], TW[1], C)
        out = out.reshape(Bs, nH, nW, TW[0], TW[1], C).transpose(0, 1, 3, 2, 4, 5).reshape(Bs, H, W, C)
        out = jnp.roll(out, shift=(SH[0], SH[1]), axis=(1, 2))
        out = out.reshape(Bs * H * W, C) @ W_proj + b_proj
        return out.reshape(Bs, H, W, C)

    def _L0_ffn_ref(x, router_w, w1, w2, w3):
        import jax, jax.numpy as jnp
        import numpy as np
        N_EXPERTS = 8
        TOP_K = 2
        B, T, C = x.shape
        flat = x.reshape(-1, C)
        logits = flat @ router_w.T
        probs = jax.nn.softmax(logits, axis=-1)
        topk_probs, topk_idx = jax.lax.top_k(probs, TOP_K)
        topk_probs = topk_probs / (jnp.sum(topk_probs, axis=-1, keepdims=True) + 1e-09)
        onehot = jax.nn.one_hot(topk_idx, N_EXPERTS, dtype=flat.dtype)
        gates = jnp.einsum('nk,nke->ne', topk_probs, onehot)
        h1 = jnp.einsum('nc,ehc->neh', flat, w1)
        h3 = jnp.einsum('nc,ehc->neh', flat, w3)
        h = jax.nn.silu(h1) * h3
        y = jnp.einsum('neh,ech->nec', h, w2)
        out = jnp.einsum('ne,nec->nc', gates, y)
        return out.reshape(B, T, C)

    def _gn(v, G=32, eps=1e-05):
        B_, H_, W_, C_ = v.shape
        g = v.reshape(B_, H_, W_, G, C_ // G)
        m = jnp.mean(g, axis=(1, 2, 4), keepdims=True)
        s = jnp.var(g, axis=(1, 2, 4), keepdims=True)
        return ((g - m) / jnp.sqrt(s + eps)).reshape(v.shape)

    def _ln_c(v, eps=1e-06):
        m = jnp.mean(v, axis=-1, keepdims=True)
        s = jnp.var(v, axis=-1, keepdims=True)
        return (v - m) / jnp.sqrt(s + eps)

    def _ln_t(v, eps=1e-05):
        m = jnp.mean(v, axis=-1, keepdims=True)
        s = jnp.var(v, axis=-1, keepdims=True)
        return (v - m) / jnp.sqrt(s + eps)

    def _to_tokens(v):
        B_, H_, W_, C_ = v.shape
        return v.reshape(B_, H_ * W_, C_)

    def _from_tokens(t, like):
        return t.reshape(like.shape)
    x = x + _L0_conv_ref(_ln_c(x), L0_conv_W_qkv, L0_conv_b_qkv, L0_conv_W_proj, L0_conv_b_proj)
    t = _to_tokens(x)
    t = t + _L0_ffn_ref(_ln_t(t), L0_ffn_router_w, L0_ffn_w1, L0_ffn_w2, L0_ffn_w3)
    x = _from_tokens(t, x)
    return x

_drawn_inputs = setup_inputs


def setup_inputs(seed=0):
    import zlib

    import numpy as np

    out = dict(_drawn_inputs(seed))
    spreads = {'L0_conv_b_qkv': (0.0, 0.1), 'L0_conv_b_proj': (0.0, 0.1)}
    factors = {'L0_conv_W_qkv': 3.032}
    for name, (base, spread) in spreads.items():
        noise = np.random.default_rng([zlib.crc32(name.encode()), seed]).standard_normal(out[name].shape)
        drawn = base * np.exp(spread * noise) if base else spread * noise
        out[name] = jnp.asarray(drawn.astype(out[name].dtype))
    for name, factor in factors.items():
        out[name] = (out[name] * factor).astype(out[name].dtype)
    return out
```

```python
from contextlib import ExitStack

import numpy as np

import concourse.bass as bass
from concourse import mybir

F32 = mybir.dt.float32
BF16 = mybir.dt.bfloat16
U32 = mybir.dt.uint32
U16 = mybir.dt.uint16
I32 = mybir.dt.int32
ALU = mybir.AluOpType
ACT = mybir.ActivationFunctionType
AX = mybir.AxisListType.X

P = 128
BATCH, SIDE, C = 4, 48, 64
HEADS, HD = 8, 8
WIN, DIL, SHIFT = 8, 2, 4
N = WIN * WIN
TOKENS = BATCH * SIDE * SIDE
TILES = TOKENS // P
PER_IMAGE = SIDE * SIDE // N
G = 4
GROUPS = TILES // G
QKV = 3 * C
E, H = 8, 682
FULL = H // P
REST = H - FULL * P
CHUNKS = FULL + 1
WCOLS = (2 * FULL + 1) * P
SLOTS = 512
SUB = SLOTS // P
REGION = TOKENS + SLOTS
MAX_TILES = 2 * TOKENS // SLOTS + E
PARTS = 3 * C // 2
ROW = PARTS + 2
EPS_C, EPS_T = 1e-6, 1e-5
BIG = -1.0e30
MASKED_PER_IMAGE = PER_IMAGE // 3
MASK_TILE = BATCH * (PER_IMAGE - MASKED_PER_IMAGE) // 2
LAG_QKV, LAG_TURN, LAG_SCORE, LAG_EXP, LAG_PT, LAG_PV, LAG_OT, LAG_PROJ = 1, 2, 3, 4, 5, 6, 7, 8
FILL_GROUPS = 5
DRAIN_GROUPS = 4
FIRST_TILES = 6 * G

K_IDENT, K_COS, K_SIN, K_PAIR, K_HEADMASK, K_VMASK, K_IOTA, K_BASE = 0, 128, 384, 640, 704, 712, 714, 722
K_COLS = 730
B_IDENT, B_TRI, B_ONES, B_MASK = 0, 128, 256, 384
B_COLS = 448


def build(nc, x_win, x_res, w_qkv, w_proj, router, w13, w2, kf, kb, tok_id, pad_rows, out):
    ctx = ExitStack()
    with ctx:
        def sb(name, shape, dt=F32):
            return ctx.enter_context(nc.sbuf_tensor(name, shape, dt))

        def sem(name):
            return ctx.enter_context(nc.semaphore(name))

        rows_dram = nc.dram_tensor("expert_rows", (E * REGION, ROW), U32, kind="Internal").ap()

        x_all = sb("x_all", [P, TILES, C])
        res_all = sb("res_all", [P, TILES, C])
        wqkv_sb = sb("wqkv_sb", [C + 1, QKV])
        wext = sb("wext", [C + 1, 2 * P + C])
        wproj_sb = sb("wproj_sb", [C + 1, C])
        router_sb = sb("router_sb", [P, 2 * E])
        w2_sb = sb("w2_sb", [P, E, CHUNKS, C])
        consts = sb("consts", [P, K_COLS])
        constb = sb("constb", [P, B_COLS], BF16)
        tok_sb = sb("tok_sb", [P, TILES], U32)
        pad_sb = sb("pad_sb", [P, SUB, ROW], U32)
        ident = consts[:, K_IDENT:K_IDENT + P]
        cos_t = consts[:, K_COS:K_COS + 2 * P].rearrange("p (a w d) -> p a w d", a=2, w=2)
        sin_t = consts[:, K_SIN:K_SIN + 2 * P].rearrange("p (a w d) -> p a w d", a=2, w=2)
        pair = consts[:, K_PAIR:K_PAIR + N]
        head_mask = consts[:, K_HEADMASK:K_HEADMASK + HEADS]
        v_mask = consts[:, K_VMASK:K_VMASK + 2]
        iota8 = consts[:, K_IOTA:K_IOTA + E]
        region_base = consts[:, K_BASE:K_BASE + E]
        ident_b = constb[:, B_IDENT:B_IDENT + P]
        tri_b = constb[:, B_TRI:B_TRI + P]
        ones_b = constb[:, B_ONES:B_ONES + P]
        mask_b = constb[:, B_MASK:B_MASK + N]
        ln1_sum = sb("ln1_sum", [P, G])
        ln1_mean = sb("ln1_mean", [P, G])
        ln1_c = sb("ln1_c", [P, G, C])
        ln1_sq = sb("ln1_sq", [P, G, C])
        ln1_var = sb("ln1_var", [P, G])
        ln1_vare = sb("ln1_vare", [P, G])
        ln1_rstd = sb("ln1_rstd", [P, G])
        xn = sb("xn", [P, G, C])
        xt = sb("xt", [C + 1, 2, 4, N])
        rope_c = sb("rope_c", [P, 2, 2, 2, C])
        rope_s = sb("rope_s", [P, 2, 2, 2, C])
        qk_bd = sb("qk_bd", [P, 2, 2, 2, C])
        qkt = sb("qkt", [P, 2, P + N])
        k_bd = sb("k_bd", [P, 2, HEADS, N])
        v_bd = sb("v_bd", [P, G, 2, 4, 18])
        smax = sb("smax", [P, 2, HEADS])
        probs = sb("probs", [P, 2, HEADS, N])
        pt = sb("pt", [P, 2, 4, P])
        rden = sb("rden", [P, 2, HEADS])
        att = sb("att", [P, 2, C])
        att_t = sb("att_t", [C + 1, 2, P])
        t_sb = sb("t_sb", [P, G, C])
        ln2_sum = sb("ln2_sum", [P, G])
        ln2_mean = sb("ln2_mean", [P, G])
        ln2_c = sb("ln2_c", [P, G, C])
        ln2_sq = sb("ln2_sq", [P, G, C])
        ln2_var = sb("ln2_var", [P, G])
        ln2_vare = sb("ln2_vare", [P, G])
        ln2_rstd = sb("ln2_rstd", [P, G])
        xn2 = sb("xn2", [P, G, C])
        xn2_t = sb("xn2_t", [P, 2, P])
        split_r = sb("split_r", [P, G, C])
        rows = sb("rows", [P, G, 2, ROW], U32)
        logits = sb("logits", [P, G, E])
        top = sb("top", [P, G, E])
        top_i = sb("top_i", [P, G, E], U32)
        top_if = sb("top_if", [P, G, 2])
        top_d = sb("top_d", [P, G, E])
        top_e = sb("top_e", [P, G, E])
        zsum = sb("zsum", [P, G])
        two = sb("two", [P, G])
        gden = sb("gden", [P, G])
        grec = sb("grec", [P, G])
        gates = sb("gates", [P, G, 2])
        chosen = sb("chosen", [P, G, 2, E])
        members = sb("members", [P, G, E], BF16)
        before = sb("before", [P, G + 1, E], BF16)
        place = sb("place", [P, G, E])
        place2 = sb("place2", [P, G, 2, E])
        slot_f = sb("slot_f", [P, G, 2])
        slot_u = sb("slot_u", [P, G, 2], U32)
        cnt_f = sb("cnt_f", [P, E])
        cnt_i = sb("cnt_i", [P, E], I32)
        til_i = sb("til_i", [P, E], I32)
        til_s = sb("til_s", [P, E], I32)
        til_f = sb("til_f", [P, E])
        til_m = sb("til_m", [P, E])
        ends_f = sb("ends_f", [P, E])
        zero8 = sb("zero8", [P, E])
        minus_half = sb("minus_half", [P, G])
        ends_i = sb("ends_i", [P, E], I32)
        padrow_f = sb("padrow_f", [P, E])
        padrow_i = sb("padrow_i", [P, E], I32)
        wraw = sb("wraw", [C, 2, WCOLS])
        wparts = sb("wparts", [C, 3, WCOLS], BF16)
        wsp = sb("wsp", [P, 2, 3, WCOLS], BF16)
        xin = sb("xin", [P, SUB, ROW], U32)
        meta = sb("meta", [P, SUB, 2], U32)
        xs = sb("xs", [P, 2, SLOTS], BF16)
        gate_h = sb("gate_h", [P, 2, SLOTS])
        hid = sb("hid", [P, 3, SLOTS])
        y_t = sb("y_t", [P, SLOTS])
        y_a = sb("y_a", [P, SUB, C])
        y_b = sb("y_b", [P, SUB, C])
        y_out = sb("y_out", [P, SUB, C])

        ps = [ctx.enter_context(nc.psum_tensor(f"bank{i}", [P, 512], F32)) for i in range(8)]
        ps_xt = ps[0][0:C, 0:P]
        ps_ot = ps[0][0:C, P:2 * P]
        ps_xn2t = ps[0][:, 2 * P:4 * P]
        ps_log = ps[0][:, 0:G * E]
        ps_qkv = [ps[1], ps[2]]
        ps_turn = ps[3][:, 0:P + N]
        ps_score = [ps[4], ps[5]]
        ps_pt = ps[6]
        ps_pv = ps[7][:, 0:72]
        ps_proj = ps[7][:, 128:128 + C]
        ps_pos = ps[7][:, 256:256 + G * E]
        ps_cnt = ps[7][:, 320:320 + E]
        ps_x = [ps[0][:, :].bitcast(BF16), ps[7][:, :].bitcast(BF16)]
        ps_h = [ps[1], ps[2]]
        ps_g = [ps[3], ps[4]]
        ps_y = ps[5]
        ps_yt = ps[6]

        c_in = sem("consts_in")
        x_in = [sem("x_in_first"), sem("x_in_rest")]
        s_half = sem("minus_half_set")
        s_dummy = sem("dummy_rows_stored")
        w_in = sem("weights_in")
        init_s = sem("init_done")
        wext_s = sem("wext_done")
        s1sum, s1mean, s1c, s1sq, s1var, s1vare, s1rstd, s1xn = [sem("ln1_" + n) for n in ("sum", "mean", "c", "sq", "var", "vare", "rstd", "xn")]
        s_xt, s_xtc = sem("xt_ps"), sem("xt_sb")
        s_qkv, s_ropem, s_qkbd, s_vbd = sem("qkv_ps"), sem("rope_mul"), sem("qk_bd_done"), sem("v_bd_done")
        s_turn, s_qktc, s_kbd = sem("turn_ps"), sem("qkt_sb"), sem("k_bd_done")
        s_score, s_max, s_sub, s_exp = sem("score_ps"), sem("max_done"), sem("sub_done"), sem("exp_done")
        s_pt, s_ptc = sem("pt_ps"), sem("pt_sb")
        s_pv, s_rden, s_att = sem("pv_ps"), sem("rden_done"), sem("att_done")
        s_ot, s_otc = sem("ot_ps"), sem("ot_sb")
        s_proj, s_t = sem("proj_ps"), sem("t_done")
        s_tout = sem("t_stored")
        s2sum, s2mean, s2c, s2sq, s2var, s2vare, s2rstd, s2xn = [sem("ln2_" + n) for n in ("sum", "mean", "c", "sq", "var", "vare", "rstd", "xn")]
        s_x2t, s_x2tc, s_log, s_logc = sem("xn2t_ps"), sem("xn2t_sb"), sem("logits_ps"), sem("logits_sb")
        s_split = sem("split_done")
        s_max8, s_idx, s_idxf, s_topd, s_tope = sem("max8"), sem("idx8"), sem("idx_f"), sem("top_d"), sem("top_e")
        s_z, s_gden, s_grec, s_gates = sem("z_two"), sem("gate_den"), sem("gate_rec"), sem("gates_done")
        s_chosen, s_members, s_before, s_bstep, s_tstep = sem("chosen_done"), sem("members_done"), sem("before_done"), sem("before_step"), sem("tile_count_step")
        s_pos, s_place, s_place2, s_slotf, s_slotu = sem("pos_ps"), sem("place"), sem("place2"), sem("slot_f"), sem("slot_u")
        s_rows, s_meta = sem("rows_done"), sem("rows_meta")
        s_scat = sem("rows_scattered")
        s_pad = sem("pads_stored")
        s_cnt, s_tile = sem("count_ps"), sem("tile_counts")
        s_wraw, s_wsp, s_wstep = [sem("wraw_in_even"), sem("wraw_in_odd")], sem("w_split"), sem("w_split_step")
        s_xin, s_x2, s_xs = sem("xin_in"), sem("x_ps"), sem("xs_sb")
        s_h, s_silu, s_hid, s_yc = sem("h_ps"), sem("silu_done"), sem("hid_done"), sem("y_chunk")
        s_ytsb, s_yt = sem("yt_sb"), sem("yt_ps")
        s_yb, s_yout, s_metain, s_added = sem("y_b"), sem("y_out_done"), sem("meta_in"), sem("y_added")

        xw_v = x_win.rearrange("(t p) c -> p t c", p=P)
        xr_v = x_res.rearrange("(t p) c -> p t c", p=P)
        out_v = out[0:TOKENS, :].rearrange("(t p) c -> p t c", p=P)

        block = ctx.enter_context(nc.Block())

        def groups(eng, body):
            def ok(t):
                return not isinstance(t, int) or 0 <= t < TILES
            turn = (MASK_TILE + LAG_SCORE) // G
            for g in range(FILL_GROUPS):
                body(g * G, ok, False)
            with eng.Fori(FILL_GROUPS * G, turn * G, G) as b:
                body(b, ok, False)
            body(turn * G, ok, None)
            with eng.Fori((turn + 1) * G, TILES - G, G) as b:
                body(b, ok, True)
            for g in range(GROUPS - 1, GROUPS + DRAIN_GROUPS):
                body(g * G, ok, True)

        def tiles_of(tg):
            if isinstance(tg, int):
                return bass.ds(tg, G)
            return bass.ds(nc.s_assert_within(tg, 0, TILES - G, skip_runtime_bounds_check_because="the loops step through whole groups"), G)

        def after(eng, s, t, back, scale=1):
            v = (t - back + 1) * scale if scale != 1 else t - back + 1
            if not isinstance(v, int):
                eng.wait_ge(s, v)
            elif v > 0:
                eng.wait_ge(s, min(v, TILES * scale))

        def hold(eng):
            eng.nop(nofuse=True)

        @block.sync
        def _(sp):
            for dst, src in ((consts[:], kf), (constb[:].bitcast(U16), kb), (tok_sb[:], tok_id), (pad_sb[:], pad_rows)):
                sp.dma_start(dst, src).then_inc(c_in, 16)
            for dst, src in ((wqkv_sb[:], w_qkv), (wproj_sb[:], w_proj), (router_sb[:], router)):
                sp.dma_start(dst, src).then_inc(w_in, 16)
            for i, (a, b) in enumerate(((0, FIRST_TILES), (FIRST_TILES, TILES))):
                sp.dma_start(x_all[:, a:b, :], xw_v[:, a:b, :]).then_inc(x_in[i], 16)
                sp.dma_start(res_all[:, a:b, :], xr_v[:, a:b, :]).then_inc(x_in[i], 16)
            sp.dma_start(w2_sb[:], w2).then_inc(w_in, 16)
            for e in range(2):
                sp.dma_start(wraw[:, e, :], w13[e]).then_inc(s_wraw[e], 16)
            sp.wait_ge(x_in[0], 32)
            sp.dma_start(out[TOKENS:TOKENS + SLOTS, :].rearrange("(c p) d -> p c d", p=P), x_all[:, 0:SUB, :]).then_inc(s_dummy, 16)

            def body(b, ok, masked):
                tg = b - 2 * G
                if ok(tg):
                    after(sp, s_t, tg, -(G - 1))
                    sp.dma_start(out_v[:, tiles_of(tg), :], t_sb[:]).then_inc(s_tout, 16)
            groups(sp, body)

            sp.wait_ge(s_tile, 2)
            for e in range(E):
                at = sp.value_load(padrow_i[0:1, e:e + 1], min_val=e * REGION, max_val=e * REGION + TOKENS)
                sp.dma_start(rows_dram[bass.ds(at, SLOTS), :].rearrange("(c p) r -> p c r", p=P),
                             pad_sb[:]).then_inc(s_pad, 16)
            sp.wait_ge(s_pad, 16 * E)
            sp.wait_ge(s_scat, 16 * 2 * TILES)
            sp.dma_start(meta[:], pad_sb[:, :, PARTS:ROW]).then_inc(s_metain, 16)
            start = 0
            for e in range(E):
                end = sp.value_load(ends_i[0:1, e:e + 1], min_val=e + 1, max_val=MAX_TILES)
                with sp.Fori(start, end) as n:
                    row0 = nc.s_assert_within((n - start) * SLOTS + e * REGION, e * REGION, e * REGION + TOKENS,
                                              skip_runtime_bounds_check_because="an expert's tiles hold at most all tokens")
                    sp.wait_ge(s_x2, n + 1)
                    sp.dma_start(xin[:], rows_dram[bass.ds(row0, SLOTS), :].rearrange("(c p) r -> p c r", p=P)).then_inc(s_xin, 16)
                    sp.wait_ge(s_added, (n + 1) * (16 * SUB))
                    sp.dma_start(meta[:], rows_dram[bass.ds(row0, SLOTS), PARTS:ROW].rearrange("(c p) r -> p c r", p=P)).then_inc(s_metain, 16)
                start = end
                if e + 2 < E:
                    sp.wait_ge(s_wstep, 4 * (e + 1))
                    sp.dma_start(wraw[:, e % 2, :], w13[e + 2]).then_inc(s_wraw[e % 2], 16)
            sp.wait_ge(s_x2, start + 1)
            sp.dma_start(xin[:], pad_sb[:]).then_inc(s_xin, 16)
            sp.wait_ge(s_tout, 16 * GROUPS)
            sp.wait_ge(s_dummy, 16)
            sp.wait_ge(s_added, (start + 1) * (16 * SUB))
            hold(sp)

        @block.tensor
        def _(pe):
            pe.wait_ge(c_in, 64)
            pe.wait_ge(wext_s, 3)
            pe.wait_ge(w_in, 64)
            pe.wait_ge(init_s, 3)

            def step(b, j, ok, masked):
                s = b + j
                t, par = s - LAG_PROJ, (j - LAG_PROJ) % 2
                if ok(t):
                    after(pe, s_otc, t, 0)
                    after(pe, s_att, s - LAG_PV, 1)
                    if not ok(s - 1 - LAG_PV):
                        after(pe, s_t, t, 1)
                    if j == 0:
                        if ok(b - 4 * G):
                            after(pe, s_place, b - 4 * G, -(G - 1))
                    pe.matmul(ps_proj, att_t[:, par, :], wproj_sb[:], start=True, stop=True).then_inc(s_proj, 1)
                t, par = s - LAG_OT, (j - LAG_OT) % 2
                if ok(t):
                    after(pe, s_att, t, 0)
                    if ok(s - 1):
                        after(pe, s_xtc, s, 1)
                    if j == 2 and ok(b - 3 * G):
                        after(pe, s_x2tc, b - 3 * G, -(G - 1))
                    if j == 3 and ok(b - 3 * G):
                        after(pe, s_logc, b - 3 * G, -(G - 1))
                    hold(pe)
                    pe.transpose(ps_ot, att[:, par, :], ident).then_inc(s_ot, 1)
                t, par = s - LAG_PV, (j - LAG_PV) % 2
                if ok(t):
                    after(pe, s_ptc, t, 0)
                    after(pe, s_vbd, t, 0)
                    if ok(s - LAG_PROJ):
                        after(pe, s_t, s - LAG_PROJ, 0)
                    else:
                        after(pe, s_att, t, 1)
                    for pr in range(4):
                        for w in range(2):
                            mm = pe.matmul(ps_pv[w * N:(w + 1) * N, pr * 18:(pr + 1) * 18],
                                           pt[:, par, pr, w * N:(w + 1) * N],
                                           v_bd[:, (j - LAG_PV) % G, w, pr, :], start=True, stop=True)
                    mm.then_inc(s_pv, 1)
                t, par = s - LAG_PT, (j - LAG_PT) % 2
                if ok(t):
                    after(pe, s_exp, t, 0)
                    after(pe, s_ptc, t, 1)
                    for pr in range(4):
                        mm = pe.transpose(ps_pt[:, pr * P:(pr + 1) * P], probs[:, par, 2 * pr:2 * pr + 2, :], ident)
                    mm.then_inc(s_pt, 1)
                t, par = s - LAG_SCORE, (j - LAG_SCORE) % 2
                if ok(t):
                    mask = masked if isinstance(masked, bool) else t >= MASK_TILE
                    after(pe, s_qktc, t, 0)
                    after(pe, s_kbd, t, 0)
                    after(pe, s_sub, t, 2)
                    mm = pe.matmul(ps_score[par][:, :], qkt[:, par, 0:P], k_bd[:, par, :, :], start=True, stop=not mask)
                    if mask:
                        mm = pe.matmul(ps_score[par][:, :], ident_b, mask_b.unsqueeze(1).to_broadcast([P, HEADS, N]), start=False, stop=True)
                    mm.then_inc(s_score, 1)
                t, par = s - LAG_TURN, (j - LAG_TURN) % 2
                if ok(t):
                    after(pe, s_qkbd, t, 0)
                    after(pe, s_qktc, t, 1)
                    pe.transpose(ps_turn[:, 0:P], qk_bd[:, par, 0, :, :], ident)
                    pe.matmul(ps_turn[:, P:P + N], qk_bd[:, par, 1, :, :], pair, start=True, stop=True).then_inc(s_turn, 1)
                t, par = s - LAG_QKV, (j - LAG_QKV) % 2
                if ok(t):
                    after(pe, s_xtc, t, 0)
                    after(pe, s_ropem, t, 2, 2)
                    after(pe, s_vbd, t, 2)
                    pe.matmul(ps_qkv[par][:, 0:2 * P], xt[:, par, 1:3, :], wext[:, 0:2 * P], start=True, stop=True)
                    for w in range(2):
                        mm = pe.matmul(ps_qkv[par][:, 2 * P + w * C:2 * P + (w + 1) * C],
                                       xt[:, par, 2 * w:2 * w + 2, :],
                                       wext[:, 2 * P:2 * P + C], start=True, stop=True)
                    mm.then_inc(s_qkv, 1)
                t, par = s, j % 2
                if ok(t):
                    after(pe, s1xn, t, 0)
                    after(pe, s_xtc, t, 1)
                    if ok(s - LAG_OT):
                        after(pe, s_otc, s - LAG_OT, 0)
                    hold(pe)
                    pe.transpose(ps_xt, xn[:, j, :], ident).then_inc(s_xt, 1)

            def last_of_bank0(s, ok):
                if ok(s):
                    after(pe, s_xtc, s, 0)
                elif ok(s - LAG_OT):
                    after(pe, s_otc, s - LAG_OT, 0)

            def body(b, ok, masked):
                for j in range(G):
                    tg = b - 4 * G
                    if j == 0 and ok(tg):
                        after(pe, s_before, tg, -(G - 1))
                        after(pe, s_att, b - LAG_PV, 1)
                        after(pe, s_t, b - LAG_PROJ, 1)
                        pe.matmul(ps_pos, tri_b, members[:], start=True, stop=False)
                        pe.matmul(ps_pos, ones_b, before[:, 0:G, :], start=False, stop=True).then_inc(s_pos, G)
                    step(b, j, ok, masked)
                    tg = b - 3 * G
                    if j == 1 and ok(tg):
                        after(pe, s2xn, tg, -(G - 1))
                        last_of_bank0(b + j, ok)
                        for m in range(2):
                            mm = pe.transpose(ps_xn2t[:, m * P:(m + 1) * P], xn2[:, 2 * m:2 * m + 2, :], ident)
                        mm.then_inc(s_x2t, G)
                    if j == 2 and ok(tg):
                        after(pe, s_x2tc, tg, -(G - 1))
                        last_of_bank0(b + j, ok)
                        for m in range(2):
                            mm = pe.matmul(ps_log[:, m * 2 * E:(m + 1) * 2 * E], xn2_t[:, m, :], router_sb[:], start=True, stop=True)
                        mm.then_inc(s_log, G)
            groups(pe, body)

            pe.wait_ge(s_before, TILES + 2)
            pe.matmul(ps_cnt, ones_b, before[:, 0, :], start=True, stop=True).then_inc(s_cnt, 1)

            def turn_rows(n):
                pe.wait_ge(s_xin, (n + 1) * 16)
                for k in range(2):
                    for c in range(SUB):
                        mm = pe.transpose(ps_x[k][:, c * P:(c + 1) * P], xin[:, c, 0:PARTS].bitcast(BF16)[:, k * C:(k + 2) * C], ident_b)
                mm.then_inc(s_x2, 1)

            def hidden(n, e, c):
                q = n * CHUNKS + c
                if c == 0:
                    pe.wait_ge(s_xs, n * 2 + 2)
                pe.wait_ge(s_hid, q + 1)
                for which in range(1 if c == FULL else 2):
                    dst = (ps_h, ps_g)[which][c % 2][:, :]
                    col = (2 * c + which) * P
                    for part in range(3):
                        mm = pe.matmul(dst, wsp[:, e % 2, part, col:col + P], xs[:, part // 2, :],
                                       start=(part == 0), stop=(part == 2))
                mm.then_inc(s_h, 1)

            def down(n, e, c):
                pe.wait_ge(s_hid, n * CHUNKS + (c + 3))
                if c == 0:
                    pe.wait_ge(s_ytsb, n + 1)
                half = c % 2
                mm = pe.matmul(ps_y[half * C:(half + 1) * C, :], w2_sb[:, e, c, :], hid[:, c % 3, :],
                               start=(c < 2), stop=(c >= CHUNKS - 2))
                mm.then_inc(s_yc, 1)

            def turn_y(k):
                pe.wait_ge(s_ytsb, k + 1)
                pe.wait_ge(s_yb, k + 1)
                for c in range(SUB):
                    mm = pe.transpose(ps_yt[:, c * P:(c + 1) * P], y_t[:, c * P:(c + 1) * P], ident)
                mm.then_inc(s_yt, 1)

            turn_rows(0)
            start = 0
            for e in range(E):
                end = pe.value_load(ends_i[0:1, e:e + 1], min_val=e + 1, max_val=MAX_TILES)
                pe.wait_ge(s_wsp, 96 * (e + 1))
                with pe.Fori(start, end) as n:
                    hidden(n, e, 0)
                    turn_y(n)
                    hidden(n, e, 1)
                    for c in range(2, CHUNKS):
                        down(n, e, c - 2)
                        hidden(n, e, c)
                    turn_rows(n + 1)
                    down(n, e, CHUNKS - 2)
                    down(n, e, CHUNKS - 1)
                start = end
            turn_y(start)

        @block.scalar
        def _(act):
            act.wait_ge(c_in, 64)
            act.wait_ge(init_s, 3)

            def step(b, j, ok):
                s = b + j
                t, par = s - LAG_OT, (j - LAG_OT) % 2
                if ok(t):
                    after(act, s_ot, t, 0)
                    after(act, s_proj, t, 2)
                    act.activation(att_t[0:C, par, :], ps_ot, ACT.Copy).then_inc(s_otc, 1)
                t, par = s - LAG_PT, (j - LAG_PT) % 2
                if ok(t):
                    after(act, s_pt, t, 0)
                    after(act, s_pv, t, 2)
                    act.activation(pt[:, par, :, :], ps_pt[:, :], ACT.Copy).then_inc(s_ptc, 1)
                t, par = s - LAG_EXP, (j - LAG_EXP) % 2
                if ok(t):
                    after(act, s_sub, t, 0)
                    act.activation(probs[:, par, :, :], probs[:, par, :, :], ACT.Exp).then_inc(s_exp, 1)
                t, par = s - LAG_TURN, (j - LAG_TURN) % 2
                if ok(t):
                    after(act, s_turn, t, 0)
                    after(act, s_score, t, 2)
                    after(act, s_kbd, t, 2)
                    act.activation(qkt[:, par, :], ps_turn, ACT.Copy).then_inc(s_qktc, 1)
                t, par = s, j % 2
                if ok(t):
                    after(act, s_xt, t, 0)
                    after(act, s_qkv, t, 2)
                    act.activation(xt[0:C, par, :, :].rearrange("p (w r) n -> p w r n", r=2),
                                   ps_xt.rearrange("p (w n) -> p w n", w=2).unsqueeze(2).to_broadcast([C, 2, 2, N]), ACT.Copy).then_inc(s_xtc, 1)

            def body(b, ok, masked):
                for j in range(G):
                    step(b, j, ok)
                    tg = b - 3 * G
                    if j == 3 and ok(tg):
                        after(act, s_topd, tg, -(G - 1))
                        act.activation(top_e[:], top_d[:], ACT.Exp).then_inc(s_tope, G)
                    if j == 1 and ok(tg):
                        after(act, s_x2t, tg, -(G - 1))
                        act.activation(xn2_t[:].rearrange("p a d -> p (a d)"), ps_xn2t, ACT.Copy).then_inc(s_x2tc, G)
                    if j == 2 and ok(tg):
                        after(act, s_log, tg, -(G - 1))
                        after(act, s_idx, tg, 1)
                        act.activation(logits[:].rearrange("p a d -> p (a d)"), ps_log, ACT.Copy).then_inc(s_logc, G)
            groups(act, body)

            def copy_rows(n):
                act.wait_ge(s_x2, n + 2)
                act.activation(xs[:, 0, :], ps_x[0][:, 0:SLOTS], ACT.Copy).then_inc(s_xs, 1)

            copy_rows(0)
            start = 0
            for e in range(E):
                end = act.value_load(ends_i[0:1, e:e + 1], min_val=e + 1, max_val=MAX_TILES)
                with act.Fori(start, end) as n:
                    for c in range(CHUNKS):
                        q = n * CHUNKS + c
                        act.wait_ge(s_h, q + 1)
                        act.wait_ge(s_hid, q + 1)
                        rows_c = P if c < FULL else C
                        act.activation(gate_h[0:rows_c, c % 2, :], ps_h[c % 2][0:rows_c, :], ACT.Silu).then_inc(s_silu, 1)
                    copy_rows(n + 1)
                    act.wait_ge(s_yc, n * CHUNKS + (CHUNKS + 3))
                    act.wait_ge(s_yt, n + 1)
                    act.activation(y_t[:], ps_y[:, :], ACT.Copy).then_inc(s_ytsb, 1)
                start = end

        @block.vector
        def _(dve):
            dve.memset(xt[C:C + 1, :, :, :], 1.0).then_inc(init_s, 1)
            dve.memset(att_t[C:C + 1, :, :], 1.0).then_inc(init_s, 1)
            dve.memset(y_t[:], 0.0).then_inc(s_ytsb, 1)
            dve.memset(zero8[:], 0.0).then_inc(s_tile, 1)
            dve.memset(before[:, 0, :], 0.0).then_inc(s_before, 1)
            dve.wait_ge(c_in, 64)
            dve.wait_ge(w_in, 64)
            for w in range(2):
                for g in range(G):
                    mm = dve.tensor_copy(v_bd[:, g, w, :, 16:18], v_mask.unsqueeze(1).to_broadcast([P, 4, 2]))
            mm.then_inc(init_s, 1)
            dve.tensor_copy(wext[:, 0:P], wqkv_sb[:, 0:P]).then_inc(wext_s, 1)
            dve.tensor_copy(wext[:, 2 * P:2 * P + C], wqkv_sb[:, P:QKV]).then_inc(wext_s, 1)
            src = wqkv_sb[:, 0:P].rearrange("p (g h d) -> p g h d", h=2, d=2)
            dst = wext[:, P:2 * P].rearrange("p (g h d) -> p g h d", h=2, d=2)
            dve.tensor_copy(dst[:, :, 0, :], src[:, :, 1, :])
            dve.tensor_copy(dst[:, :, 1, :], src[:, :, 0, :]).then_inc(wext_s, 1)
            dve.wait_ge(x_in[0], 32)

            def norm1_sums(tg):
                after(dve, s1mean, tg, 1)
                dve.reduce_sum(ln1_sum[:], x_all[:, tiles_of(tg), :], AX).then_inc(s1sum, G)
                after(dve, s1sum, tg, -(G - 1))
                after(dve, s1c, tg, 1)
                dve.tensor_scalar(ln1_mean[:], ln1_sum[:], 1.0 / C, None, ALU.mult).then_inc(s1mean, G)

            def norm1_scale(tg):
                after(dve, s1sq, tg, -(G - 1))
                dve.reduce_sum(ln1_var[:], ln1_sq[:], AX).then_inc(s1var, G)
                after(dve, s1var, tg, -(G - 1))
                after(dve, s1rstd, tg, 1)
                dve.tensor_scalar(ln1_vare[:], ln1_var[:], 1.0 / C, EPS_C, ALU.mult, ALU.add).then_inc(s1vare, G)

            def norm2_sums(tg):
                after(dve, s_t, tg, -(G - 1))
                dve.reduce_sum(ln2_sum[:], t_sb[:], AX).then_inc(s2sum, G)
                after(dve, s2sum, tg, -(G - 1))
                after(dve, s2c, tg, 1)
                dve.tensor_scalar(ln2_mean[:], ln2_sum[:], 1.0 / C, None, ALU.mult).then_inc(s2mean, G)

            def norm2_scale(tg):
                after(dve, s2sq, tg, -(G - 1))
                dve.reduce_sum(ln2_var[:], ln2_sq[:], AX).then_inc(s2var, G)
                after(dve, s2var, tg, -(G - 1))
                after(dve, s2rstd, tg, 1)
                dve.tensor_scalar(ln2_vare[:], ln2_var[:], 1.0 / C, EPS_T, ALU.mult, ALU.add).then_inc(s2vare, G)

            def pick(tg):
                after(dve, s_logc, tg, -(G - 1))
                hold(dve)
                for g in range(G):
                    mm = dve.max(top[:, g, :], logits[:, g, :])
                mm.then_inc(s_max8, G)
                after(dve, s_max8, tg, -(G - 1))
                hold(dve)
                for g in range(G):
                    mm = dve.max_index(top_i[:, g, :], top[:, g, :], logits[:, g, :])
                mm.then_inc(s_idx, G)
                dve.tensor_tensor(top_d[:], top[:], top[:, :, 0:1].to_broadcast([P, G, E]), ALU.subtract).then_inc(s_topd, G)
                after(dve, s_idx, tg, -(G - 1))
                dve.tensor_copy(top_if[:], top_i[:, :, 0:2]).then_inc(s_idxf, G)
                after(dve, s_idxf, tg, -(G - 1))
                dve.tensor_tensor(chosen[:], iota8.unsqueeze(1).unsqueeze(1).to_broadcast([P, G, 2, E]),
                                  top_if[:].unsqueeze(3).to_broadcast([P, G, 2, E]), ALU.is_equal).then_inc(s_chosen, G)
                after(dve, s_chosen, tg, -(G - 1))
                after(dve, s_pos, tg, 1)
                dve.tensor_tensor(members[:], chosen[:, :, 0, :], chosen[:, :, 1, :], ALU.add).then_inc(s_members, G)
                after(dve, s_members, tg, -(G - 1))
                if not isinstance(tg, int) or tg > 0:
                    dve.wait_ge(s_before, tg + 1)
                    dve.tensor_copy(before[:, 0, :], before[:, G, :]).then_inc(s_bstep, 1)
                else:
                    dve.wait_ge(s_before, 1)
                    dve.engine_nop().then_inc(s_bstep, 1)
                for g in range(G):
                    dve.wait_ge(s_bstep, tg + g + 1)
                    dve.tensor_tensor(before[:, g + 1, :], before[:, g, :], members[:, g, :], ALU.add).then_inc(s_bstep if g < G - 1 else s_before, 1 if g < G - 1 else G)

            def weigh(tg):
                after(dve, s_tope, tg, -(G - 1))
                dve.reduce_sum(zsum[:], top_e[:], AX)
                dve.reduce_sum(two[:], top_e[:, :, 0:2], AX).then_inc(s_z, G)
                after(dve, s_z, tg, -(G - 1))
                dve.scalar_tensor_tensor(out=gden[:], in0=zsum[:], scalar=1e-9, in1=two[:], op0=ALU.mult, op1=ALU.add).then_inc(s_gden, G)
                after(dve, s_gden, tg, -(G - 1))
                dve.reciprocal(grec[:], gden[:]).then_inc(s_grec, G)
                after(dve, s_grec, tg, -(G - 1))
                after(dve, s_meta, tg, 1)
                dve.tensor_tensor(gates[:], top_e[:, :, 0:2], grec[:].unsqueeze(2).to_broadcast([P, G, 2]), ALU.mult).then_inc(s_gates, G)

            def find_slots(tg):
                after(dve, s_pos, tg, -(G - 1))
                dve.tensor_tensor(place[:].rearrange("p g e -> p (g e)"), ps_pos, region_base.unsqueeze(1).to_broadcast([P, G, E]), ALU.add).then_inc(s_place, G)
                after(dve, s_place, tg, -(G - 1))
                dve.tensor_tensor(place2[:], chosen[:], place[:].unsqueeze(2).to_broadcast([P, G, 2, E]), ALU.mult).then_inc(s_place2, G)
                after(dve, s_place2, tg, -(G - 1))
                dve.reduce_sum(slot_f[:], place2[:], AX).then_inc(s_slotf, G)
                after(dve, s_slotf, tg, -(G - 1))
                after(dve, s_scat, tg, 1, 32)
                dve.tensor_copy(slot_u[:], slot_f[:]).then_inc(s_slotu, G)

            def step(b, j, ok):
                s = b + j
                t, par = s - LAG_PROJ, (j - LAG_PROJ) % 2
                if ok(t):
                    after(dve, s_proj, t, 0)
                    if j == 0:
                        after(dve, s2c, t, 1)
                        if not isinstance(t, int) or t > 0:
                            dve.wait_ge(s_tout, t * (16 // G))
                    dve.tensor_tensor(t_sb[:, j, :], ps_proj, res_all[:, t, :], ALU.add).then_inc(s_t, 1)
                t, par = s - LAG_PV, (j - LAG_PV) % 2
                if ok(t):
                    after(dve, s_pv, t, 0)
                    o = ps_pv.rearrange("p (a d) -> p a d", d=18)
                    dve.reciprocal(rden[:, par, :].rearrange("p (a d) -> p a d", d=2), o[:, :, 16:18]).then_inc(s_rden, 1)
                    after(dve, s_rden, t, 0)
                    after(dve, s_ot, t, 2)
                    dve.tensor_tensor(att[:, par, :].rearrange("p (a h d) -> p a h d", h=2, d=HD),
                                      o[:, :, 0:16].rearrange("p a (h d) -> p a h d", d=HD),
                                      rden[:, par, :].rearrange("p (a h) -> p a h", h=2).unsqueeze(3).to_broadcast([P, 4, 2, HD]),
                                      ALU.mult).then_inc(s_att, 1)
                t, par = s - 3, (j - 3) % 2
                if ok(t):
                    after(dve, s_qkv, t, 0)
                    after(dve, s_pv, t, 4)
                    for w in range(2):
                        mm = dve.tensor_tensor(v_bd[:, (j - 3) % G, w, :, 0:16].rearrange("p a (h d) -> p a h d", d=HD),
                                               ps_qkv[par][:, 2 * P + w * C:2 * P + (w + 1) * C].rearrange("p (a h d) -> p a h d", h=2, d=HD),
                                               v_mask.unsqueeze(1).unsqueeze(3).to_broadcast([P, 4, 2, HD]), ALU.mult)
                    mm.then_inc(s_vbd, 1)
                t, par = s - LAG_EXP, (j - LAG_EXP) % 2
                if ok(t):
                    after(dve, s_score, t, 0)
                    sc = ps_score[par][:, :].rearrange("p (h k) -> p h k", k=N)
                    dve.reduce_max(smax[:, par, :], sc, AX).then_inc(s_max, 1)
                    after(dve, s_max, t, 0)
                    after(dve, s_pt, t, 2)
                    dve.tensor_tensor(probs[:, par, :, :], sc, smax[:, par, :].unsqueeze(2).to_broadcast([P, HEADS, N]), ALU.subtract).then_inc(s_sub, 1)
                t, par = s - LAG_QKV, (j - LAG_QKV) % 2
                if ok(t):
                    after(dve, s_qkv, t, 0)
                    after(dve, s_qkbd, t, 2)
                    for dst, col, table in ((rope_c, 0, cos_t), (rope_s, P, sin_t)):
                        dve.tensor_tensor(dst[:, par, :, :, :], ps_qkv[par][:, col:col + P].rearrange("p (a d) -> p a d", a=2)
                                          .unsqueeze(2).to_broadcast([P, 2, 2, C]), table, ALU.mult).then_inc(s_ropem, 1)
                t, par = s - LAG_TURN, (j - LAG_TURN) % 2
                if ok(t):
                    after(dve, s_qktc, t, 0)
                    after(dve, s_score, t, 2)
                    dve.tensor_tensor(k_bd[:, par, :, :], qkt[:, par, P:P + N].unsqueeze(1).to_broadcast([P, HEADS, N]),
                                      head_mask.unsqueeze(2).to_broadcast([P, HEADS, N]), ALU.mult).then_inc(s_kbd, 1)

            norm1_sums(0)
            norm1_scale(0)

            def body(b, ok, masked):
                if isinstance(b, int) and b == FIRST_TILES - 2 * G:
                    dve.wait_ge(x_in[1], 32)
                for j in range(G):
                    if j == 0 and ok(b - 4 * G):
                        find_slots(b - 4 * G)
                    step(b, j, ok)
                    if j == 0 and ok(b - 4 * G):
                        weigh(b - 4 * G)
                    if j == 0 and ok(b - 3 * G):
                        norm2_scale(b - 3 * G)
                    if j == 0 and ok(b + G):
                        norm1_sums(b + G)
                    if j == 2 and ok(b + G):
                        norm1_scale(b + G)
                    if j == 3 and ok(b - 2 * G):
                        norm2_sums(b - 2 * G)
                    if j == 3 and ok(b - 3 * G):
                        pick(b - 3 * G)
            groups(dve, body)

            dve.wait_ge(s_before, TILES + 1)
            dve.tensor_copy(before[:, 0, :], before[:, G, :]).then_inc(s_before, 1)
            dve.wait_ge(s_cnt, 1)
            dve.tensor_copy(cnt_f[:], ps_cnt).then_inc(s_tstep, 1)
            dve.wait_ge(s_tstep, 1)
            dve.tensor_scalar(til_f[:], cnt_f[:], float(SLOTS - 1), None, ALU.add).then_inc(s_tstep, 1)
            dve.tensor_tensor(padrow_f[:], cnt_f[:], region_base, ALU.add).then_inc(s_tstep, 1)
            dve.wait_ge(s_tstep, 3)
            dve.tensor_copy(til_i[:], til_f[:]).then_inc(s_tstep, 1)
            dve.tensor_copy(padrow_i[:], padrow_f[:]).then_inc(s_tstep, 1)
            dve.wait_ge(s_tstep, 5)
            dve.tensor_scalar(til_s[:], til_i[:], 9, None, ALU.arith_shift_right).then_inc(s_tstep, 1)
            dve.wait_ge(s_tstep, 6)
            dve.tensor_copy(til_f[:], til_s[:]).then_inc(s_tstep, 1)
            dve.wait_ge(s_tstep, 7)
            dve.tensor_scalar(til_m[:], til_f[:], 1.0, None, ALU.max).then_inc(s_tstep, 1)
            dve.wait_ge(s_tstep, 8)
            dve.tensor_tensor_scan(ends_f[:], til_m[:], zero8[:], 0.0, ALU.add, ALU.add).then_inc(s_tstep, 1)
            dve.wait_ge(s_tstep, 9)
            dve.tensor_copy(ends_i[:], ends_f[:]).then_inc(s_tile, 1)
            dve.engine_nop().then_inc(s_hid, 2)
            dve.engine_nop().then_inc(s_x2, 1)
            dve.engine_nop().then_inc(s_yb, 1)
            dve.engine_nop().then_inc(s_yout, 1)

            def copy_rows(n):
                dve.wait_ge(s_x2, n + 2)
                dve.tensor_copy(xs[:, 1, :], ps_x[1][:, 0:SLOTS]).then_inc(s_xs, 1)

            def tail(k):
                dve.wait_ge(s_yt, k + 1)
                dve.wait_ge(s_metain, (k + 1) * 16)
                dve.wait_ge(s_yout, k + 1)
                y4 = ps_yt[:, :].rearrange("p (c h d) -> p c h d", h=2, d=C)
                gate = meta[:].bitcast(F32)[:, :, 0:1].to_broadcast([P, SUB, C])
                dve.tensor_tensor(y_a[:], y4[:, :, 0, :], gate, ALU.mult)
                dve.tensor_tensor(y_b[:], y4[:, :, 1, :], gate, ALU.mult).then_inc(s_yb, 1)

            copy_rows(0)
            start = 0
            for e in range(E):
                end = dve.value_load(ends_i[0:1, e:e + 1], min_val=e + 1, max_val=MAX_TILES)
                with dve.Fori(start, end) as n:
                    for c in range(CHUNKS):
                        q = n * CHUNKS + c
                        dve.wait_ge(s_silu, q + 1)
                        dve.wait_ge(s_yc, q + 1)
                        if c < FULL:
                            dve.tensor_tensor(hid[:, c % 3, :], gate_h[:, c % 2, :], ps_g[c % 2][:, :], ALU.mult).then_inc(s_hid, 1)
                        else:
                            dve.tensor_tensor(hid[0:C, c % 3, :], gate_h[0:C, c % 2, :], ps_h[c % 2][C:2 * C, :], ALU.mult).then_inc(s_hid, 1)
                        if c == 0:
                            tail(n)
                    copy_rows(n + 1)
                start = end
            tail(start)

        @block.gpsimd
        def _(pool):
            pool.memset(minus_half[:], -0.5).then_inc(s_half, 1)
            pool.wait_ge(c_in, 64)
            pool.wait_ge(x_in[0], 32)
            pool.wait_ge(init_s, 3)
            pool.wait_ge(s_half, 1)

            def split_weights(e):
                raw, k = wraw[:, e % 2, :], e * 4
                hi, mid, lo = [wparts[:, i, :] for i in range(3)]
                pool.wait_ge(s_wraw[e % 2], 16 * (e // 2 + 1))
                if e > 0:
                    pool.wait_ge(s_wsp, 96 * e)
                pool.tensor_copy(hi, raw).then_inc(s_wstep, 1)
                pool.wait_ge(s_wstep, k + 1)
                pool.tensor_tensor(raw, raw, hi, ALU.subtract).then_inc(s_wstep, 1)
                pool.wait_ge(s_wstep, k + 2)
                pool.tensor_copy(mid, raw).then_inc(s_wstep, 1)
                pool.wait_ge(s_wstep, k + 3)
                pool.tensor_tensor(lo, raw, mid, ALU.subtract).then_inc(s_wstep, 1)
                pool.wait_ge(s_wstep, k + 4)
                for i, (upper, lower) in enumerate(((hi, mid), (mid, hi), (lo, hi))):
                    pool.dma_start(wsp[0:C, e % 2, i, :], upper).then_inc(s_wsp, 16)
                    pool.dma_start(wsp[C:2 * C, e % 2, i, :], lower).then_inc(s_wsp, 16)

            def center(x, mean, c, sq, s_mean, s_c, s_sq, s_var, s_norm, tg):
                after(pool, s_mean, tg, -(G - 1))
                after(pool, s_norm, tg, 1)
                pool.tensor_tensor(c[:], x, mean[:].unsqueeze(2).to_broadcast([P, G, C]), ALU.subtract).then_inc(s_c, G)
                after(pool, s_c, tg, -(G - 1))
                after(pool, s_var, tg, 1)
                pool.tensor_tensor(sq[:], c[:], c[:], ALU.mult).then_inc(s_sq, G)

            def scale1(tg, half):
                a = half * 2
                if half == 0:
                    after(pool, s1vare, tg, -(G - 1))
                    pool.tensor_tensor(ln1_rstd[:], ln1_vare[:], minus_half[:], ALU.pow).then_inc(s1rstd, G)
                after(pool, s1rstd, tg, -(G - 1))
                after(pool, s_xt, tg - G + a + 1, 0)
                pool.tensor_tensor(xn[:, a:a + 2, :], ln1_c[:, a:a + 2, :], ln1_rstd[:, a:a + 2].unsqueeze(2).to_broadcast([P, 2, C]), ALU.mult).then_inc(s1xn, 2)

            def scatter(tg):
                for g in range(G):
                    for k in range(2):
                        pool.indirect_dma_start(rows_dram, bass.IndirectOffsetOnAxis(ap=slot_u[:, g, k:k + 1], axis=0),
                                                rows[:, g, k, :], None).then_inc(s_scat, 16)

            def split_rows(tg):
                after(pool, s2xn, tg, -(G - 1))
                after(pool, s_scat, tg, 1, 32)
                hold(pool)
                mid, hi, lo = [rows[:, :, 0, k * C // 2:(k + 1) * C // 2].bitcast(BF16) for k in range(3)]
                pool.tensor_copy(hi, xn2[:]).then_inc(s_split, 1)
                pool.wait_ge(s_split, tg + 1)
                pool.tensor_tensor(split_r[:], xn2[:], hi, ALU.subtract).then_inc(s_split, 1)
                pool.wait_ge(s_split, tg + 2)
                hold(pool)
                pool.tensor_copy(mid, split_r[:]).then_inc(s_split, 1)
                pool.wait_ge(s_split, tg + 3)
                pool.tensor_tensor(lo, split_r[:], mid, ALU.subtract).then_inc(s_split, 1)
                pool.wait_ge(s_split, tg + 4)
                hold(pool)
                pool.tensor_copy(rows[:, :, 1, 0:PARTS], rows[:, :, 0, 0:PARTS]).then_inc(s_rows, G)

            def fill_meta(tg):
                after(pool, s_gates, tg, -(G - 1))
                hold(pool)
                m = rows[:, :, :, PARTS:ROW]
                pool.tensor_copy(m.bitcast(F32)[:, :, :, 0], gates[:])
                pool.tensor_copy(m[:, :, :, 1], tok_sb[:, tiles_of(tg)].unsqueeze(2).to_broadcast([P, G, 2])).then_inc(s_meta, G)

            center(x_all[:, 0:G, :], ln1_mean, ln1_c, ln1_sq, s1mean, s1c, s1sq, s1var, s1xn, 0)
            scale1(0, 0)
            scale1(0, 1)

            def body(b, ok, masked):
                if isinstance(b, int) and b == FIRST_TILES - 2 * G:
                    pool.wait_ge(x_in[1], 32)
                for j in range(G):
                    t, par = b + j - LAG_QKV, (j - LAG_QKV) % 2
                    if ok(t):
                        after(pool, s_ropem, t, 0, 2)
                        after(pool, s_turn, t, 2)
                        pool.tensor_tensor(qk_bd[:, par, :, :, :], rope_c[:, par, :, :, :], rope_s[:, par, :, :, :], ALU.add).then_inc(s_qkbd, 1)
                    tg = b - 4 * G
                    if j == 1 and ok(tg):
                        fill_meta(tg)
                        after(pool, s_slotu, tg, -(G - 1))
                        after(pool, s_meta, tg, -(G - 1))
                        hold(pool)
                        scatter(tg)
                    tg = b - 3 * G
                    if j == 0 and ok(tg):
                        after(pool, s2vare, tg, -(G - 1))
                        pool.tensor_tensor(ln2_rstd[:], ln2_vare[:], minus_half[:], ALU.pow).then_inc(s2rstd, G)
                        after(pool, s2rstd, tg, -(G - 1))
                        after(pool, s_x2t, tg, 1)
                        pool.tensor_tensor(xn2[:], ln2_c[:], ln2_rstd[:].unsqueeze(2).to_broadcast([P, G, C]), ALU.mult).then_inc(s2xn, G)
                    if j == 2 and ok(tg):
                        split_rows(tg)
                    tg = b + G
                    if j == 1 and ok(tg):
                        center(x_all[:, tiles_of(tg), :], ln1_mean, ln1_c, ln1_sq, s1mean, s1c, s1sq, s1var, s1xn, tg)
                    if j == 2 and ok(tg):
                        scale1(tg, 0)
                    if j == 3 and ok(tg):
                        scale1(tg, 1)
                    tg = b - 2 * G
                    if j == 3 and ok(tg):
                        center(t_sb[:], ln2_mean, ln2_c, ln2_sq, s2mean, s2c, s2sq, s2var, s2xn, tg)
            groups(pool, body)
            pool.engine_nop().then_inc(s_yc, 3)
            split_weights(0)

            def add_rows(k):
                pool.wait_ge(s_yb, k + 2)
                pool.tensor_tensor(y_out[:], y_a[:], y_b[:], ALU.add).then_inc(s_yout, 1)
                pool.wait_ge(s_yout, k + 2)
                hold(pool)
                for c in range(SUB):
                    pool.indirect_dma_start(out, bass.IndirectOffsetOnAxis(ap=meta[:, c, 1:2], axis=0),
                                            y_out[:, c, :], None, compute_op=ALU.add).then_inc(s_added, 16)
                pool.wait_ge(s_added, (k + 1) * (16 * SUB))
                hold(pool)

            pool.wait_ge(s_tile, 2)
            pool.wait_ge(s_tout, 16 * GROUPS)
            pool.wait_ge(s_dummy, 16)
            start = 0
            for e in range(E):
                end = pool.value_load(ends_i[0:1, e:e + 1], min_val=e + 1, max_val=MAX_TILES)
                if e + 1 < E:
                    pool.wait_ge(s_yc, start * CHUNKS + 3)
                    hold(pool)
                    split_weights(e + 1)
                with pool.Fori(start, end) as n:
                    add_rows(n)
                start = end
            add_rows(start)


def window_order():
    n_side = SIDE // (WIN * DIL)
    wins, masked = [], []
    for img in range(BATCH):
        for w in range(PER_IMAGE):
            (masked if w >= PER_IMAGE - MASKED_PER_IMAGE else wins).append((img, w))
    src, dst = [], []
    for img, w in wins + masked:
        block, d = divmod(w, DIL * DIL)
        bh, bw = divmod(block, n_side)
        dh, dw = divmod(d, DIL)
        base = (img * PER_IMAGE + w) * N
        for n in range(N):
            i, j = divmod(n, WIN)
            row = (bh * WIN * DIL + i * DIL + dh + SHIFT) % SIDE
            col = (bw * WIN * DIL + j * DIL + dw + SHIFT) % SIDE
            src.append(base + n)
            dst.append((img * SIDE + row) * SIDE + col)
    return np.array(src), np.array(dst)


def constants():
    kf = np.zeros((P, K_COLS), np.float32)
    kf[:, K_IDENT:K_IDENT + P] = np.eye(P)
    half = HD // 4
    inv = (1.0 / 10000.0 ** (np.arange(half, dtype=np.float32) / half)).astype(np.float32)
    tok = np.arange(P) % N
    for ax, pos in enumerate((tok // WIN, tok % WIN)):
        ang = pos[:, None].astype(np.float32) * inv
        for hh in range(2):
            for d in range(half):
                for head in range(HEADS):
                    col = head * HD + ax * (HD // 2) + hh * half + d
                    for which, scale in enumerate((HD ** -0.5, 1.0)):
                        own = np.arange(P), which * 2 * C + (np.arange(P) // N) * C + col
                        kf[own[0], K_COS + own[1]] = np.cos(ang[:, d]) * scale
                        kf[own[0], K_SIN + own[1]] = np.sin(ang[:, d]) * scale * (1, -1)[hh == 0]
    kf[np.arange(P), K_PAIR + np.arange(P) % N] = 1
    kf[np.arange(P), K_HEADMASK + (np.arange(P) % C) // HD] = 1
    kf[np.arange(P), K_VMASK + np.arange(P) // N] = 1
    kf[:, K_IOTA:K_IOTA + E] = np.arange(E)
    kf[:, K_BASE:K_BASE + E] = np.arange(E) * REGION
    kb = np.zeros((P, B_COLS), np.float32)
    kb[:, B_IDENT:B_IDENT + P] = np.eye(P)
    kb[:, B_TRI:B_TRI + P] = np.arange(P)[:, None] < np.arange(P)[None, :]
    kb[:, B_ONES:B_ONES + P] = 1
    region = np.digitize(np.arange(N) // WIN, (WIN // 2, WIN // 2 + SHIFT // DIL))
    kb[:, B_MASK:B_MASK + N] = np.where(region[tok][:, None] != region[None, :], BIG, 0)
    tok_id = (np.arange(TILES)[None, :] * P + np.arange(P)[:, None]).astype(np.uint32)
    pad = np.zeros((P, SUB, ROW), np.uint32)
    pad[:, :, ROW - 1] = TOKENS + np.arange(SUB)[None, :] * P + np.arange(P)[:, None]
    return kf, (kb.view(np.uint32) >> 16).astype(np.uint16), tok_id, pad


def kernel(x, L0_conv_W_qkv, L0_conv_b_qkv, L0_conv_W_proj, L0_conv_b_proj, L0_ffn_router_w, L0_ffn_w1, L0_ffn_w2, L0_ffn_w3):
    import concourse.bacc as bacc
    from concourse.bass_utils import run_bass_kernel_spmd

    x = np.asarray(x)
    src, dst = window_order()
    flat = x.reshape(TOKENS, C)
    w1, w2, w3 = (np.asarray(a) for a in (L0_ffn_w1, L0_ffn_w2, L0_ffn_w3))
    w13 = np.zeros((E, C, WCOLS), np.float32)
    for c in range(FULL):
        w13[:, :, 2 * c * P:(2 * c + 1) * P] = w1[:, c * P:(c + 1) * P, :].transpose(0, 2, 1)
        w13[:, :, (2 * c + 1) * P:(2 * c + 2) * P] = w3[:, c * P:(c + 1) * P, :].transpose(0, 2, 1)
    w13[:, :, 2 * FULL * P:2 * FULL * P + REST] = w1[:, FULL * P:, :].transpose(0, 2, 1)
    w13[:, :, 2 * FULL * P + C:2 * FULL * P + C + REST] = w3[:, FULL * P:, :].transpose(0, 2, 1)
    w2t = np.zeros((P, E, CHUNKS, C), np.float32)
    for c in range(CHUNKS):
        k = min(P, H - c * P)
        w2t[0:k, :, c, :] = w2[:, :, c * P:c * P + k].transpose(2, 0, 1)
    router = np.zeros((P, 2 * E), np.float32)
    router[0:C, 0:E] = np.asarray(L0_ffn_router_w).T
    router[C:2 * C, E:2 * E] = np.asarray(L0_ffn_router_w).T
    kf, kb, tok_id, pad = constants()
    arrays = {
        "x_win": flat[src], "x_res": flat[dst],
        "w_qkv": np.concatenate([np.asarray(L0_conv_W_qkv), np.asarray(L0_conv_b_qkv)[None, :]], 0),
        "w_proj": np.concatenate([np.asarray(L0_conv_W_proj), np.asarray(L0_conv_b_proj)[None, :]], 0),
        "router": router, "w13": w13, "w2": w2t, "kf": kf, "kb": kb, "tok_id": tok_id, "pad_rows": pad,
    }
    nc = bacc.Bacc("TRN2", target_bir_lowering=False, num_devices=1)
    args = {n: nc.dram_tensor(n, a.shape, mybir.dt.from_np(a.dtype), kind="ExternalInput").ap() for n, a in arrays.items()}
    out = nc.dram_tensor("out", (TOKENS + SLOTS, C), F32, kind="ExternalOutput").ap()
    build(nc, out=out, **args)
    r = run_bass_kernel_spmd(nc, [arrays], core_ids=[0])
    rows = np.asarray(r.results[0]["out"])
    y = np.empty((TOKENS, C), np.float32)
    y[dst] = rows[0:TOKENS]
    return y.reshape(x.shape)
```

```python
from contextlib import ExitStack

import numpy as np

import concourse.bass as bass
from concourse import mybir

F32 = mybir.dt.float32
BF16 = mybir.dt.bfloat16
U32 = mybir.dt.uint32
U16 = mybir.dt.uint16
I32 = mybir.dt.int32
ALU = mybir.AluOpType
ACT = mybir.ActivationFunctionType
AX = mybir.AxisListType.X

P = 128
BATCH, SIDE, C = 4, 48, 64
HEADS, HD = 8, 8
WIN, DIL, SHIFT = 8, 2, 4
N = WIN * WIN
TOKENS = BATCH * SIDE * SIDE
TILES = TOKENS // P
PER_IMAGE = SIDE * SIDE // N
G = 4
GROUPS = TILES // G
QKV = 3 * C
E, H = 8, 682
FULL = H // P
REST = H - FULL * P
CHUNKS = FULL + 1
WCOLS = (2 * FULL + 1) * P
SLOTS = 512
SUB = SLOTS // P
REGION = TOKENS + SLOTS
MAX_TILES = 2 * TOKENS // SLOTS + E
PARTS = 3 * C // 2
ROW = PARTS + 2
EPS_C, EPS_T = 1e-6, 1e-5
BIG = -1.0e30
MASKED_PER_IMAGE = PER_IMAGE // 3
MASK_TILE = BATCH * (PER_IMAGE - MASKED_PER_IMAGE) // 2
LAG_QKV, LAG_ROPE, LAG_TURN, LAG_V, LAG_SCORE, LAG_MAX, LAG_PT, LAG_PV, LAG_OT, LAG_PROJ = 1, 2, 3, 3, 4, 5, 6, 7, 8, 8
FILL_GROUPS = 5
DRAIN_GROUPS = 4
LAST_SPLIT = FILL_GROUPS + E - 1
assert (LAST_SPLIT + 1) * G == MASK_TILE + LAG_SCORE
FIRST_TILES = 6 * G

K_IDENT, K_COS, K_SIN, K_PAIR, K_HEADMASK, K_VMASK, K_IOTA, K_BASE = 0, 128, 384, 640, 704, 712, 714, 722
K_COLS = 730
B_IDENT, B_TRI, B_ONES, B_MASK = 0, 128, 256, 384
B_COLS = 448


def build(nc, x_win, x_res, w_qkv, w_proj, router, w13, w2, kf, kb, tok_id, pad_rows, out):
    ctx = ExitStack()
    with ctx:
        def sb(name, shape, dt=F32):
            return ctx.enter_context(nc.sbuf_tensor(name, shape, dt))

        def sem(name):
            return ctx.enter_context(nc.semaphore(name))

        rows_dram = nc.dram_tensor("expert_rows", (E * REGION, ROW), U32, kind="Internal").ap()

        x_all = sb("x_all", [P, TILES, C])
        res_all = sb("res_all", [P, TILES, C])
        wqkv_sb = sb("wqkv_sb", [C + 1, QKV])
        wext = sb("wext", [C + 1, 2 * P + C])
        wproj_sb = sb("wproj_sb", [C + 1, C])
        router_sb = sb("router_sb", [P, 2 * E])
        w2_sb = sb("w2_sb", [P, E, CHUNKS, C])
        consts = sb("consts", [P, K_COLS])
        constb = sb("constb", [P, B_COLS], BF16)
        tok_sb = sb("tok_sb", [P, TILES], U32)
        pad_sb = sb("pad_sb", [P, SUB, ROW], U32)
        ident = consts[:, K_IDENT:K_IDENT + P]
        cos_t = consts[:, K_COS:K_COS + 2 * P].rearrange("p (a w d) -> p a w d", a=2, w=2)
        sin_t = consts[:, K_SIN:K_SIN + 2 * P].rearrange("p (a w d) -> p a w d", a=2, w=2)
        pair = consts[:, K_PAIR:K_PAIR + N]
        head_mask = consts[:, K_HEADMASK:K_HEADMASK + HEADS]
        v_mask = consts[:, K_VMASK:K_VMASK + 2]
        iota8 = consts[:, K_IOTA:K_IOTA + E]
        region_base = consts[:, K_BASE:K_BASE + E]
        ident_b = constb[:, B_IDENT:B_IDENT + P]
        tri_b = constb[:, B_TRI:B_TRI + P]
        ones_b = constb[:, B_ONES:B_ONES + P]
        mask_b = constb[:, B_MASK:B_MASK + N]
        ln1_sum = sb("ln1_sum", [P, G])
        ln1_mean = sb("ln1_mean", [P, G])
        ln1_c = sb("ln1_c", [P, G, C])
        ln1_sq = sb("ln1_sq", [P, G, C])
        ln1_var = sb("ln1_var", [P, G])
        ln1_vare = sb("ln1_vare", [P, G])
        ln1_rstd = sb("ln1_rstd", [P, G])
        xn = sb("xn", [P, G, C])
        xt = sb("xt", [C + 1, 2, 4, N])
        rope_c = sb("rope_c", [P, 2, 2, C])
        rope_s = sb("rope_s", [P, 2, 2, C])
        qk_bd = sb("qk_bd", [P, 2, 2, 2, C])
        qkt = sb("qkt", [P, 2, P + N])
        k_bd = sb("k_bd", [P, 2, HEADS, N])
        v_bd = sb("v_bd", [P, G, 2, 4, 18])
        smax = sb("smax", [P, 2, HEADS])
        probs = sb("probs", [P, 2, HEADS, N])
        pt = sb("pt", [P, 2, 4, P])
        rden = sb("rden", [P, 2, HEADS])
        att = sb("att", [P, 2, C])
        att_t = sb("att_t", [C + 1, 2, P])
        ln2_sum = sb("ln2_sum", [P, G])
        ln2_mean = sb("ln2_mean", [P, G])
        ln2_c = sb("ln2_c", [P, G, C])
        ln2_sq = sb("ln2_sq", [P, G, C])
        ln2_var = sb("ln2_var", [P, G])
        ln2_vare = sb("ln2_vare", [P, G])
        ln2_rstd = sb("ln2_rstd", [P, G])
        xn2 = sb("xn2", [P, G, C])
        xn2_t = sb("xn2_t", [P, 2, P])
        split_r = sb("split_r", [P, G, C])
        parts = sb("parts", [P, G, 3, C], BF16)
        rows = sb("rows", [P, G, 2, ROW], U32)
        logits = sb("logits", [P, G, E])
        top = sb("top", [P, G, E])
        top_i = sb("top_i", [P, G, E], U32)
        top_if = sb("top_if", [P, G, 2])
        top_d = sb("top_d", [P, G, E])
        top_e = sb("top_e", [P, G, E])
        zsum = sb("zsum", [P, G])
        two = sb("two", [P, G])
        gden = sb("gden", [P, G])
        grec = sb("grec", [P, G])
        gates = sb("gates", [P, G, 2])
        chosen = sb("chosen", [P, G, 2, E])
        members = sb("members", [P, G, E], BF16)
        before = sb("before", [P, G + 1, E], BF16)
        place = sb("place", [P, G, E])
        place2 = sb("place2", [P, G, 2, E])
        slot_f = sb("slot_f", [P, G, 2])
        slot_u = sb("slot_u", [P, G, 2], U32)
        cnt_f = sb("cnt_f", [P, E])
        cnt_i = sb("cnt_i", [P, E], I32)
        til_i = sb("til_i", [P, E], I32)
        til_s = sb("til_s", [P, E], I32)
        til_f = sb("til_f", [P, E])
        til_m = sb("til_m", [P, E])
        ends_f = sb("ends_f", [P, E])
        zero8 = sb("zero8", [P, E])
        minus_half = sb("minus_half", [P, G])
        ends_i = sb("ends_i", [P, E], I32)
        padrow_f = sb("padrow_f", [P, E])
        padrow_i = sb("padrow_i", [P, E], I32)
        wraw = sb("wraw", [C, WCOLS])
        wsp = sb("wsp", [P, E, 3, WCOLS], BF16)
        xin = sb("xin", [P, SUB, ROW], U32)
        meta = sb("meta", [P, SUB, 2], U32)
        meta_next = sb("meta_next", [P, SUB, 2], U32)
        xs = sb("xs", [P, 2, SLOTS], BF16)
        gate_h = sb("gate_h", [P, 2, SLOTS])
        hid = sb("hid", [P, 3, SLOTS])
        y_t = sb("y_t", [P, SLOTS])
        y_a = sb("y_a", [P, SUB, C])
        y_b = sb("y_b", [P, SUB, C])
        y_out = sb("y_out", [P, SUB, C])

        ps = [ctx.enter_context(nc.psum_tensor(f"bank{i}", [P, 512], F32)) for i in range(8)]
        ps_xt = ps[0][0:C, 0:P]
        ps_ot = ps[0][0:C, P:2 * P]
        ps_xn2t = ps[0][:, 2 * P:4 * P]
        ps_log = ps[0][:, 0:G * E]
        ps_qkv = [ps[1], ps[2]]
        ps_turn = ps[3][:, 0:P + N]
        ps_score = [ps[4], ps[5]]
        ps_pt = ps[6]
        ps_pv = ps[7][:, 0:72]
        ps_proj = ps[7][:, 128:128 + C]
        ps_pos = ps[7][:, 256:256 + G * E]
        ps_cnt = ps[7][:, 320:320 + E]
        ps_x = [ps[0][:, :].bitcast(BF16), ps[7][:, :].bitcast(BF16)]
        ps_h = [ps[1], ps[2]]
        ps_g = [ps[3], ps[4]]
        ps_y = ps[5]
        ps_yt = ps[6]

        c_in = sem("consts_in")
        x_in = [sem("x_in_first"), sem("x_in_rest")]
        s_half = sem("minus_half_set")
        s_dummy = sem("dummy_rows_stored")
        w_in, w2_in = sem("weights_in"), sem("w2_in")
        init_s = sem("init_done")
        wext_s = sem("wext_done")
        s1sum, s1mean, s1c, s1sq, s1var, s1vare, s1rstd, s1xn = [sem("ln1_" + n) for n in ("sum", "mean", "c", "sq", "var", "vare", "rstd", "xn")]
        s_xt, s_xtc = sem("xt_ps"), sem("xt_sb")
        s_qkv, s_ropem, s_qkbd, s_vbd = sem("qkv_ps"), sem("rope_mul"), sem("qk_bd_done"), sem("v_bd_done")
        s_turn, s_qktc, s_kbd = sem("turn_ps"), sem("qkt_sb"), sem("k_bd_done")
        s_score, s_max, s_sub, s_exp = sem("score_ps"), sem("max_done"), sem("sub_done"), sem("exp_done")
        s_pt, s_ptc = sem("pt_ps"), sem("pt_sb")
        s_pv, s_rden, s_att = sem("pv_ps"), sem("rden_done"), sem("att_done")
        s_ot, s_otc = sem("ot_ps"), sem("ot_sb")
        s_proj, s_t = sem("proj_ps"), sem("t_done")
        s_tout = sem("t_stored")
        s2sum, s2mean, s2c, s2sq, s2var, s2vare, s2rstd, s2xn = [sem("ln2_" + n) for n in ("sum", "mean", "c", "sq", "var", "vare", "rstd", "xn")]
        s_x2t, s_x2tc, s_log, s_logc = sem("xn2t_ps"), sem("xn2t_sb"), sem("logits_ps"), sem("logits_sb")
        s_hi, s_rest, s_mid, s_lo = sem("high_part"), sem("rest_of_high"), sem("middle_part"), sem("low_part")
        s_max8, s_idx, s_idxf, s_topd, s_tope = sem("max8"), sem("idx8"), sem("idx_f"), sem("top_d"), sem("top_e")
        s_z, s_gden, s_grec, s_gates = sem("z_two"), sem("gate_den"), sem("gate_rec"), sem("gates_done")
        s_chosen, s_members, s_before, s_bstep, s_tstep = sem("chosen_done"), sem("members_done"), sem("before_done"), sem("before_step"), sem("tile_count_step")
        s_pos, s_place, s_place2, s_slotf, s_slotu = sem("pos_ps"), sem("place"), sem("place2"), sem("slot_f"), sem("slot_u")
        s_rows, s_meta = sem("rows_done"), sem("rows_meta")
        s_scat = sem("rows_scattered")
        s_pad = sem("pads_stored")
        s_cnt, s_tile = sem("count_ps"), sem("tile_counts")
        s_wraw, s_wlow = sem("wraw_in"), sem("w_lower_halves")
        s_whi, s_wrest, s_wmid, s_wlo = sem("w_high"), sem("w_rest_of_high"), sem("w_middle"), sem("w_low")
        s_xin, s_x2, s_xs = sem("xin_in"), sem("x_ps"), sem("xs_sb")
        s_h, s_silu, s_hid, s_yc = sem("h_ps"), sem("silu_done"), sem("hid_done"), sem("y_chunk")
        s_ytsb, s_yt = sem("yt_sb"), sem("yt_ps")
        s_yb, s_yout, s_added = sem("y_b"), sem("y_out_done"), sem("y_added")
        s_tailmeta, s_nextmeta = sem("tail_meta"), sem("next_meta")

        w13_rows = w13.rearrange("e c f -> (e c) f")
        wsp_flat = wsp[:].rearrange("p e i f -> p (e i f)")
        out_v = out[0:TOKENS, :].rearrange("(t p) c -> p t c", p=P)

        block = ctx.enter_context(nc.Block())

        def groups(eng, body):
            def ok(t):
                return not isinstance(t, int) or 0 <= t < TILES
            for g in range(FILL_GROUPS):
                body(g * G, ok, False)
            with eng.Fori(FILL_GROUPS * G, LAST_SPLIT * G, G) as b:
                body(b, ok, False)
            body(LAST_SPLIT * G, ok, False)
            with eng.Fori((LAST_SPLIT + 1) * G, TILES - G, G) as b:
                body(b, ok, True)
            for g in range(GROUPS - 1, GROUPS + DRAIN_GROUPS):
                body(g * G, ok, True)

        def tiles_of(tg):
            if isinstance(tg, int):
                return bass.ds(tg, G)
            return bass.ds(nc.s_assert_within(tg, 0, TILES - G, skip_runtime_bounds_check_because="the loops step through whole groups"), G)

        def split_group(b, masked):
            if not masked and (not isinstance(b, int) or b == LAST_SPLIT * G):
                return b - FILL_GROUPS * G
            return None

        def within(v, last):
            if isinstance(v, int):
                return v
            return nc.s_assert_within(v, 0, last, skip_runtime_bounds_check_because="the first loop has a group for every expert but the last")

        def wsp_part(wt, i):
            col = within(wt * (3 * WCOLS // G) + i * WCOLS, E * 3 * WCOLS - WCOLS)
            return wsp_flat[0:C, bass.ds(col, WCOLS)]

        def after(eng, s, t, back, scale=1):
            v = (t - back + 1) * scale if scale != 1 else t - back + 1
            if not isinstance(v, int):
                eng.wait_ge(s, v)
            elif v > 0:
                eng.wait_ge(s, min(v, TILES * scale))

        def hold(eng):
            eng.nop(nofuse=True)

        @block.sync
        def _(sp):
            sp.dma_start(consts[:], kf).then_inc(c_in, 16)
            sp.dma_start(wqkv_sb[:], w_qkv).then_inc(w_in, 16)
            for i, (a, b) in enumerate(((0, FIRST_TILES), (FIRST_TILES, TILES))):
                sp.dma_start(x_all[:, a:b, :], x_win[:, a:b, :]).then_inc(x_in[i], 16)
                if i == 0:
                    for dst, src in ((constb[:].bitcast(U16), kb), (tok_sb[:], tok_id), (pad_sb[:], pad_rows)):
                        sp.dma_start(dst, src).then_inc(c_in, 16)
                    for dst, src in ((wproj_sb[:], w_proj), (router_sb[:], router)):
                        sp.dma_start(dst, src).then_inc(w_in, 16)
                sp.dma_start(res_all[:, a:b, :], x_res[:, a:b, :]).then_inc(x_in[i], 16)
            sp.dma_start(w2_sb[:], w2).then_inc(w2_in, 16)
            sp.dma_start(wraw[:], w13[0]).then_inc(s_wraw, 16)
            sp.wait_ge(x_in[0], 32)
            sp.dma_start(out[TOKENS:TOKENS + SLOTS, :].rearrange("(c p) d -> p c d", p=P), x_all[:, 0:SUB, :]).then_inc(s_dummy, 16)

            def body(b, ok, masked):
                wt = split_group(b, masked)
                if wt is not None:
                    sp.wait_ge(s_wmid, wt + G)
                    at = within(wt * (3 * WCOLS // G), (E - 1) * 3 * WCOLS)
                    sp.dma_start(wsp_flat[C:2 * C, bass.ds(at, WCOLS)], wsp_part(wt, 1)).then_inc(s_wlow, 16)
                    for i in range(1, 3):
                        at = within(wt * (3 * WCOLS // G) + i * WCOLS, E * 3 * WCOLS - WCOLS)
                        sp.dma_start(wsp_flat[C:2 * C, bass.ds(at, WCOLS)], wsp_part(wt, 0)).then_inc(s_wlow, 16)
                    if not isinstance(b, int):
                        sp.wait_ge(s_wlo, wt + G)
                        row = within(wt * (C // G) + C, (E - 1) * C)
                        sp.dma_start(wraw[:], w13_rows[bass.ds(row, C), :]).then_inc(s_wraw, 16)
                tg = b - 2 * G
                if ok(tg):
                    after(sp, s_t, tg, -(G - 1))
                    sp.dma_start(out_v[:, tiles_of(tg), :], res_all[:, tiles_of(tg), :]).then_inc(s_tout, 16)
            groups(sp, body)

            sp.wait_ge(s_tile, 2)
            for e in range(E):
                at = sp.value_load(padrow_i[0:1, e:e + 1], min_val=e * REGION, max_val=e * REGION + TOKENS)
                sp.dma_start(rows_dram[bass.ds(at, SLOTS), :].rearrange("(c p) r -> p c r", p=P),
                             pad_sb[:]).then_inc(s_pad, 16)
            sp.wait_ge(s_pad, 16 * E)
            sp.wait_ge(s_scat, 16 * 2 * TILES)
            start = 0
            for e in range(E):
                end = sp.value_load(ends_i[0:1, e:e + 1], min_val=e + 1, max_val=MAX_TILES)
                with sp.Fori(start, end) as n:
                    row0 = nc.s_assert_within((n - start) * SLOTS + e * REGION, e * REGION, e * REGION + TOKENS,
                                              skip_runtime_bounds_check_because="an expert's tiles hold at most all tokens")
                    sp.wait_ge(s_x2, n + 1)
                    sp.wait_ge(s_nextmeta, n + 1)
                    sp.dma_start(xin[:], rows_dram[bass.ds(row0, SLOTS), :].rearrange("(c p) r -> p c r", p=P)).then_inc(s_xin, 16)
                start = end
            sp.wait_ge(s_x2, start + 1)
            sp.wait_ge(s_nextmeta, start + 1)
            sp.dma_start(xin[:], pad_sb[:]).then_inc(s_xin, 16)
            sp.wait_ge(s_tout, 16 * GROUPS)
            sp.wait_ge(s_dummy, 16)
            sp.wait_ge(s_added, (start + 1) * (16 * SUB))
            hold(sp)

        @block.tensor
        def _(pe):
            pe.wait_ge(c_in, 64)
            pe.wait_ge(wext_s, 3)
            pe.wait_ge(w_in, 48)
            pe.wait_ge(init_s, 3)

            def step(b, j, ok, masked):
                s = b + j
                t, par = s - LAG_PV, (j - LAG_PV) % 2
                if ok(t):
                    after(pe, s_ptc, t, 0)
                    after(pe, s_vbd, t, 0)
                    after(pe, s_t, s - LAG_PROJ, 1)
                    after(pe, s_att, t, 1)
                    if j == 1 and ok(b - 4 * G):
                        after(pe, s_place, b - 4 * G, -(G - 1))
                    for pr in range(4):
                        for w in range(2):
                            mm = pe.matmul(ps_pv[w * N:(w + 1) * N, pr * 18:(pr + 1) * 18],
                                           pt[:, par, pr, w * N:(w + 1) * N],
                                           v_bd[:, (j - LAG_PV) % G, w, pr, :], start=True, stop=True)
                    mm.then_inc(s_pv, 1)
                t, par = s - LAG_PT, (j - LAG_PT) % 2
                if ok(t):
                    after(pe, s_exp, t, 0)
                    after(pe, s_ptc, t, 1)
                    for pr in range(4):
                        mm = pe.transpose(ps_pt[:, pr * P:(pr + 1) * P], probs[:, par, 2 * pr:2 * pr + 2, :], ident)
                    mm.then_inc(s_pt, 1)
                t, par = s - LAG_OT, (j - LAG_OT) % 2
                if ok(t):
                    after(pe, s_att, t, 0)
                    after(pe, s_xtc, s, 1)
                    if j == 2 and ok(b - 3 * G):
                        after(pe, s_x2tc, b - 3 * G, -(G - 1))
                    if j == 3 and ok(b - 3 * G):
                        after(pe, s_logc, b - 3 * G, -(G - 1))
                    hold(pe)
                    pe.transpose(ps_ot, att[:, par, :], ident).then_inc(s_ot, 1)
                t, par = s - LAG_SCORE, (j - LAG_SCORE) % 2
                if ok(t):
                    after(pe, s_qktc, t, 0)
                    after(pe, s_kbd, t, 0)
                    after(pe, s_sub, t, 2)
                    mm = pe.matmul(ps_score[par][:, :], qkt[:, par, 0:P], k_bd[:, par, :, :], start=True, stop=not masked)
                    if masked:
                        mm = pe.matmul(ps_score[par][:, :], ident_b, mask_b.unsqueeze(1).to_broadcast([P, HEADS, N]), start=False, stop=True)
                    mm.then_inc(s_score, 1)
                t, par = s - LAG_PROJ, (j - LAG_PROJ) % 2
                if ok(t):
                    after(pe, s_otc, t, 0)
                    after(pe, s_att, s - LAG_PV, 0)
                    after(pe, s_t, t, 1)
                    if j == 1 and ok(b - 4 * G):
                        after(pe, s_place, b - 4 * G, -(G - 1))
                    pe.matmul(ps_proj, att_t[:, par, :], wproj_sb[:], start=True, stop=True).then_inc(s_proj, 1)
                tg = b - 3 * G
                if j == 1 and ok(tg):
                    after(pe, s2xn, tg, -(G - 1))
                    after(pe, s_xtc, s, 1)
                    after(pe, s_otc, s - LAG_OT, 0)
                    for m in range(2):
                        mm = pe.transpose(ps_xn2t[:, m * P:(m + 1) * P], xn2[:, 2 * m:2 * m + 2, :], ident)
                    mm.then_inc(s_x2t, G)
                if j == 2 and ok(tg):
                    after(pe, s_x2tc, tg, -(G - 1))
                    after(pe, s_xtc, s, 1)
                    after(pe, s_otc, s - LAG_OT, 0)
                    for m in range(2):
                        mm = pe.matmul(ps_log[:, m * 2 * E:(m + 1) * 2 * E], xn2_t[:, m, :], router_sb[:], start=True, stop=True)
                    mm.then_inc(s_log, G)
                t, par = s - LAG_TURN, (j - LAG_TURN) % 2
                if ok(t):
                    after(pe, s_qkbd, t, 0)
                    after(pe, s_qktc, t, 1)
                    pe.transpose(ps_turn[:, 0:P], qk_bd[:, par, 0, :, :], ident)
                    pe.matmul(ps_turn[:, P:P + N], qk_bd[:, par, 1, :, :], pair, start=True, stop=True).then_inc(s_turn, 1)
                t, par = s - LAG_QKV, (j - LAG_QKV) % 2
                if ok(t):
                    after(pe, s_xtc, t, 0)
                    after(pe, s_ropem, t, 2, 2)
                    after(pe, s_vbd, t, 2)
                    pe.matmul(ps_qkv[par][:, 0:2 * P], xt[:, par, 1:3, :], wext[:, 0:2 * P], start=True, stop=True)
                    for w in range(2):
                        mm = pe.matmul(ps_qkv[par][:, 2 * P + w * C:2 * P + (w + 1) * C],
                                       xt[:, par, 2 * w:2 * w + 2, :],
                                       wext[:, 2 * P:2 * P + C], start=True, stop=True)
                    mm.then_inc(s_qkv, 1)
                t, par = s, j % 2
                if ok(t):
                    after(pe, s1xn, t, 0)
                    after(pe, s_xtc, t, 1)
                    after(pe, s_otc, s - LAG_OT, 0)
                    if j == 1 and ok(b - 3 * G):
                        after(pe, s_x2tc, b - 3 * G, -(G - 1))
                    if j == 2 and ok(b - 3 * G):
                        after(pe, s_logc, b - 3 * G, -(G - 1))
                    hold(pe)
                    pe.transpose(ps_xt, xn[:, j, :], ident).then_inc(s_xt, 1)
                tg = b - 4 * G
                if j == 0 and ok(tg):
                    after(pe, s_before, tg, -(G - 1))
                    after(pe, s_att, s - LAG_PV, 0)
                    after(pe, s_t, s - LAG_PROJ, 0)
                    pe.matmul(ps_pos, tri_b, members[:], start=True, stop=False)
                    pe.matmul(ps_pos, ones_b, before[:, 0:G, :], start=False, stop=True).then_inc(s_pos, G)

            def body(b, ok, masked):
                for j in range(G):
                    step(b, j, ok, masked)
            groups(pe, body)

            pe.wait_ge(s_before, TILES + 2)
            pe.matmul(ps_cnt, ones_b, before[:, 0, :], start=True, stop=True).then_inc(s_cnt, 1)

            def turn_rows(n):
                pe.wait_ge(s_xin, (n + 1) * 16)
                for k in range(2):
                    for c in range(SUB):
                        mm = pe.transpose(ps_x[k][:, c * P:(c + 1) * P], xin[:, c, 0:PARTS].bitcast(BF16)[:, k * C:(k + 2) * C], ident_b)
                mm.then_inc(s_x2, 1)

            def hidden(n, e, c):
                q = n * CHUNKS + c
                if c == 0:
                    pe.wait_ge(s_xs, n * 2 + 2)
                pe.wait_ge(s_hid, q + 1)
                for which in range(1 if c == FULL else 2):
                    dst = (ps_h, ps_g)[which][c % 2][:, :]
                    col = (2 * c + which) * P
                    for part in range(3):
                        mm = pe.matmul(dst, wsp[:, e, part, col:col + P], xs[:, part // 2, :],
                                       start=(part == 0), stop=(part == 2))
                mm.then_inc(s_h, 1)

            def down(n, e, c):
                pe.wait_ge(s_hid, n * CHUNKS + (c + 3))
                if c == 0:
                    pe.wait_ge(s_ytsb, n + 1)
                half = c % 2
                mm = pe.matmul(ps_y[half * C:(half + 1) * C, :], w2_sb[:, e, c, :], hid[:, c % 3, :],
                               start=(c < 2), stop=(c >= CHUNKS - 2))
                mm.then_inc(s_yc, 1)

            def turn_y(k):
                pe.wait_ge(s_ytsb, k + 1)
                pe.wait_ge(s_yb, k + 1)
                for c in range(SUB):
                    mm = pe.transpose(ps_yt[:, c * P:(c + 1) * P], y_t[:, c * P:(c + 1) * P], ident)
                mm.then_inc(s_yt, 1)

            pe.wait_ge(s_wlow, 16 * 3 * E)
            pe.wait_ge(s_wlo, G * E)
            pe.wait_ge(w2_in, 16)
            turn_rows(0)
            start = 0
            for e in range(E):
                end = pe.value_load(ends_i[0:1, e:e + 1], min_val=e + 1, max_val=MAX_TILES)
                with pe.Fori(start, end) as n:
                    hidden(n, e, 0)
                    turn_y(n)
                    hidden(n, e, 1)
                    for c in range(2, CHUNKS):
                        down(n, e, c - 2)
                        hidden(n, e, c)
                    turn_rows(n + 1)
                    down(n, e, CHUNKS - 2)
                    down(n, e, CHUNKS - 1)
                start = end
            turn_y(start)

        @block.scalar
        def _(act):
            act.wait_ge(c_in, 64)
            act.wait_ge(init_s, 3)

            def step(b, j, ok):
                s = b + j
                t, par = s - LAG_PT, (j - LAG_PT) % 2
                if ok(t):
                    after(act, s_sub, t, 0)
                    act.activation(probs[:, par, :, :], probs[:, par, :, :], ACT.Exp).then_inc(s_exp, 1)
                    after(act, s_pt, t, 0)
                    after(act, s_pv, t, 2)
                    act.activation(pt[:, par, :, :], ps_pt[:, :], ACT.Copy).then_inc(s_ptc, 1)
                t, par = s - LAG_OT, (j - LAG_OT) % 2
                if ok(t):
                    after(act, s_ot, t, 0)
                    after(act, s_proj, t, 2)
                    act.activation(att_t[0:C, par, :], ps_ot, ACT.Copy).then_inc(s_otc, 1)
                t, par = s - LAG_V, (j - LAG_V) % 2
                if ok(t):
                    after(act, s_qkv, t, 0)
                    after(act, s_ropem, t, 0, 2)
                    after(act, s_pv, t, 4)
                    v = ps_qkv[par][:, 2 * P:2 * P + 2 * C].rearrange("p (w a d) -> p w a d", w=2, d=2 * HD)
                    for h in range(2):
                        mm = act.activation(v_bd[:, (j - LAG_V) % G, :, :, h * HD:(h + 1) * HD], v[:, :, :, h * HD:(h + 1) * HD],
                                            ACT.Copy, scale=v_mask[:, h:h + 1])
                    mm.then_inc(s_vbd, 1)
                tg = b - 3 * G
                if j == 1 and ok(tg):
                    after(act, s_x2t, tg, -(G - 1))
                    act.activation(xn2_t[:].rearrange("p a d -> p (a d)"), ps_xn2t, ACT.Copy).then_inc(s_x2tc, G)
                if j == 2 and ok(tg):
                    after(act, s_log, tg, -(G - 1))
                    after(act, s_idx, tg, 1)
                    act.activation(logits[:].rearrange("p a d -> p (a d)"), ps_log, ACT.Copy).then_inc(s_logc, G)
                t, par = s - LAG_TURN, (j - LAG_TURN) % 2
                if ok(t):
                    after(act, s_turn, t, 0)
                    after(act, s_score, t, 2)
                    after(act, s_kbd, t, 2)
                    act.activation(qkt[:, par, :], ps_turn, ACT.Copy).then_inc(s_qktc, 1)
                t, par = s, j % 2
                if ok(t):
                    after(act, s_xt, t, 0)
                    after(act, s_qkv, t, 2)
                    act.activation(xt[0:C, par, :, :].rearrange("p (w r) n -> p w r n", r=2),
                                   ps_xt.rearrange("p (w n) -> p w n", w=2).unsqueeze(2).to_broadcast([C, 2, 2, N]), ACT.Copy).then_inc(s_xtc, 1)

            def body(b, ok, masked):
                for j in range(G):
                    step(b, j, ok)
                    tg = b - 4 * G
                    if j == 0 and ok(tg):
                        after(act, s_topd, tg, -(G - 1))
                        act.activation(top_e[:], top_d[:], ACT.Exp).then_inc(s_tope, G)
                        after(act, s_lo, tg, -(G - 1))
                        after(act, s_scat, tg, 1, 32)
                        for k in range(2):
                            mm = act.activation(rows[:, :, k, 0:PARTS].bitcast(BF16), parts[:].rearrange("p g i d -> p g (i d)"), ACT.Copy)
                        mm.then_inc(s_rows, G)
                    tg = b - 3 * G
                    if j == 1 and ok(tg):
                        after(act, s2xn, tg, -(G - 1))
                        after(act, s_rows, tg, 1)
                        act.activation(parts[:, :, 1, :], xn2[:], ACT.Copy).then_inc(s_hi, G)
                    if j == 2 and ok(tg):
                        after(act, s_rest, tg, -(G - 1))
                        act.activation(parts[:, :, 0, :], split_r[:], ACT.Copy).then_inc(s_mid, G)
                    wt = split_group(b, masked)
                    if j == 1 and wt is not None:
                        act.wait_ge(s_wraw, wt * (16 // G) + 16)
                        act.activation(wsp_part(wt, 0), wraw[:], ACT.Copy).then_inc(s_whi, G)
                    if j == 2 and wt is not None:
                        act.wait_ge(s_wrest, wt + G)
                        act.activation(wsp_part(wt, 1), wraw[:], ACT.Copy).then_inc(s_wmid, G)
            groups(act, body)

            def copy_rows(n):
                act.wait_ge(s_x2, n + 2)
                act.activation(xs[:, 0, :], ps_x[0][:, 0:SLOTS], ACT.Copy).then_inc(s_xs, 1)

            copy_rows(0)
            start = 0
            for e in range(E):
                end = act.value_load(ends_i[0:1, e:e + 1], min_val=e + 1, max_val=MAX_TILES)
                with act.Fori(start, end) as n:
                    for c in range(CHUNKS):
                        q = n * CHUNKS + c
                        act.wait_ge(s_h, q + 1)
                        act.wait_ge(s_hid, q + 1)
                        rows_c = P if c < FULL else C
                        act.activation(gate_h[0:rows_c, c % 2, :], ps_h[c % 2][0:rows_c, :], ACT.Silu).then_inc(s_silu, 1)
                    copy_rows(n + 1)
                    act.wait_ge(s_yc, n * CHUNKS + (CHUNKS + 3))
                    act.wait_ge(s_yt, n + 1)
                    act.activation(y_t[:], ps_y[:, :], ACT.Copy).then_inc(s_ytsb, 1)
                start = end

        @block.vector
        def _(dve):
            dve.memset(xt[C:C + 1, :, :, :], 1.0).then_inc(init_s, 1)
            dve.memset(att_t[C:C + 1, :, :], 1.0).then_inc(init_s, 1)
            dve.memset(y_t[:], 0.0).then_inc(s_ytsb, 1)
            dve.memset(zero8[:], 0.0).then_inc(s_tile, 1)
            dve.memset(before[:, 0, :], 0.0).then_inc(s_before, 1)
            dve.wait_ge(c_in, 64)
            dve.wait_ge(w_in, 48)
            for w in range(2):
                for g in range(G):
                    mm = dve.tensor_copy(v_bd[:, g, w, :, 16:18], v_mask.unsqueeze(1).to_broadcast([P, 4, 2]))
            mm.then_inc(init_s, 1)
            dve.tensor_copy(wext[:, 0:P], wqkv_sb[:, 0:P]).then_inc(wext_s, 1)
            dve.tensor_copy(wext[:, 2 * P:2 * P + C], wqkv_sb[:, P:QKV]).then_inc(wext_s, 1)
            src = wqkv_sb[:, 0:P].rearrange("p (g h d) -> p g h d", h=2, d=2)
            dst = wext[:, P:2 * P].rearrange("p (g h d) -> p g h d", h=2, d=2)
            dve.tensor_copy(dst[:, :, 0, :], src[:, :, 1, :])
            dve.tensor_copy(dst[:, :, 1, :], src[:, :, 0, :]).then_inc(wext_s, 1)
            dve.wait_ge(x_in[0], 32)

            def norm1_sums(tg):
                after(dve, s1mean, tg, 1)
                dve.reduce_sum(ln1_sum[:], x_all[:, tiles_of(tg), :], AX).then_inc(s1sum, G)
                after(dve, s1sum, tg, -(G - 1))
                after(dve, s1c, tg, 1)
                dve.tensor_scalar(ln1_mean[:], ln1_sum[:], 1.0 / C, None, ALU.mult).then_inc(s1mean, G)

            def norm1_scale(tg):
                after(dve, s1sq, tg, -(G - 1))
                dve.reduce_sum(ln1_var[:], ln1_sq[:], AX).then_inc(s1var, G)
                after(dve, s1var, tg, -(G - 1))
                after(dve, s1rstd, tg, 1)
                dve.tensor_scalar(ln1_vare[:], ln1_var[:], 1.0 / C, EPS_C, ALU.mult, ALU.add).then_inc(s1vare, G)

            def norm2_sums(tg):
                after(dve, s_t, tg, -(G - 1))
                dve.reduce_sum(ln2_sum[:], res_all[:, tiles_of(tg), :], AX).then_inc(s2sum, G)
                after(dve, s2sum, tg, -(G - 1))
                after(dve, s2c, tg, 1)
                dve.tensor_scalar(ln2_mean[:], ln2_sum[:], 1.0 / C, None, ALU.mult).then_inc(s2mean, G)

            def norm2_scale(tg):
                after(dve, s2sq, tg, -(G - 1))
                dve.reduce_sum(ln2_var[:], ln2_sq[:], AX).then_inc(s2var, G)
                after(dve, s2var, tg, -(G - 1))
                after(dve, s2rstd, tg, 1)
                dve.tensor_scalar(ln2_vare[:], ln2_var[:], 1.0 / C, EPS_T, ALU.mult, ALU.add).then_inc(s2vare, G)

            def pick(tg):
                after(dve, s_logc, tg, -(G - 1))
                hold(dve)
                for g in range(G):
                    mm = dve.max(top[:, g, :], logits[:, g, :])
                mm.then_inc(s_max8, G)
                after(dve, s_max8, tg, -(G - 1))
                hold(dve)
                for g in range(G):
                    mm = dve.max_index(top_i[:, g, :], top[:, g, :], logits[:, g, :])
                mm.then_inc(s_idx, G)
                dve.tensor_tensor(top_d[:], top[:], top[:, :, 0:1].to_broadcast([P, G, E]), ALU.subtract).then_inc(s_topd, G)
                after(dve, s_idx, tg, -(G - 1))
                dve.tensor_copy(top_if[:], top_i[:, :, 0:2]).then_inc(s_idxf, G)
                after(dve, s_idxf, tg, -(G - 1))
                dve.tensor_tensor(chosen[:], iota8.unsqueeze(1).unsqueeze(1).to_broadcast([P, G, 2, E]),
                                  top_if[:].unsqueeze(3).to_broadcast([P, G, 2, E]), ALU.is_equal).then_inc(s_chosen, G)
                after(dve, s_chosen, tg, -(G - 1))
                after(dve, s_pos, tg, 1)
                dve.tensor_tensor(members[:], chosen[:, :, 0, :], chosen[:, :, 1, :], ALU.add).then_inc(s_members, G)
                after(dve, s_members, tg, -(G - 1))
                if not isinstance(tg, int) or tg > 0:
                    dve.wait_ge(s_before, tg + 1)
                    dve.tensor_copy(before[:, 0, :], before[:, G, :]).then_inc(s_bstep, 1)
                else:
                    dve.wait_ge(s_before, 1)
                    dve.engine_nop().then_inc(s_bstep, 1)
                for g in range(G):
                    dve.wait_ge(s_bstep, tg + g + 1)
                    dve.tensor_tensor(before[:, g + 1, :], before[:, g, :], members[:, g, :], ALU.add).then_inc(s_bstep if g < G - 1 else s_before, 1 if g < G - 1 else G)

            def weigh(tg):
                after(dve, s_tope, tg, -(G - 1))
                dve.reduce_sum(zsum[:], top_e[:], AX)
                dve.reduce_sum(two[:], top_e[:, :, 0:2], AX).then_inc(s_z, G)
                after(dve, s_z, tg, -(G - 1))
                dve.scalar_tensor_tensor(out=gden[:], in0=zsum[:], scalar=1e-9, in1=two[:], op0=ALU.mult, op1=ALU.add).then_inc(s_gden, G)
                after(dve, s_gden, tg, -(G - 1))
                dve.reciprocal(grec[:], gden[:]).then_inc(s_grec, G)
                after(dve, s_grec, tg, -(G - 1))
                after(dve, s_meta, tg, 1)
                dve.tensor_tensor(gates[:], top_e[:, :, 0:2], grec[:].unsqueeze(2).to_broadcast([P, G, 2]), ALU.mult).then_inc(s_gates, G)

            def find_slots(tg):
                after(dve, s_pos, tg, -(G - 1))
                dve.tensor_tensor(place[:].rearrange("p g e -> p (g e)"), ps_pos, region_base.unsqueeze(1).to_broadcast([P, G, E]), ALU.add).then_inc(s_place, G)
                after(dve, s_place, tg, -(G - 1))
                after(dve, s_slotu, tg, 1)
                dve.tensor_tensor(place2[:], chosen[:], place[:].unsqueeze(2).to_broadcast([P, G, 2, E]), ALU.mult).then_inc(s_place2, G)
                after(dve, s_place2, tg, -(G - 1))
                dve.reduce_sum(slot_f[:], place2[:], AX).then_inc(s_slotf, G)
                after(dve, s_slotf, tg, -(G - 1))

            def step(b, j, ok):
                s = b + j
                t, par = s - LAG_SCORE, (j - LAG_SCORE) % 2
                if ok(t):
                    after(dve, s_qktc, t, 0)
                    after(dve, s_score, t, 2)
                    dve.tensor_tensor(k_bd[:, par, :, :], qkt[:, par, P:P + N].unsqueeze(1).to_broadcast([P, HEADS, N]),
                                      head_mask.unsqueeze(2).to_broadcast([P, HEADS, N]), ALU.mult).then_inc(s_kbd, 1)
                t, par = s - LAG_PV, (j - LAG_PV) % 2
                if ok(t):
                    after(dve, s_pv, t, 0)
                    o = ps_pv.rearrange("p (a d) -> p a d", d=18)
                    dve.reciprocal(rden[:, par, :].rearrange("p (a d) -> p a d", d=2), o[:, :, 16:18]).then_inc(s_rden, 1)
                    after(dve, s_rden, t, 0)
                    after(dve, s_ot, t, 2)
                    dve.tensor_tensor(att[:, par, :].rearrange("p (a h d) -> p a h d", h=2, d=HD),
                                      o[:, :, 0:16].rearrange("p a (h d) -> p a h d", d=HD),
                                      rden[:, par, :].rearrange("p (a h) -> p a h", h=2).unsqueeze(3).to_broadcast([P, 4, 2, HD]),
                                      ALU.mult).then_inc(s_att, 1)
                t, par = s - LAG_ROPE, (j - LAG_ROPE) % 2
                if ok(t):
                    after(dve, s_qkv, t, 0)
                    after(dve, s_qkbd, t, 1)
                    for dst, col, table in ((rope_c, 0, cos_t), (rope_s, P, sin_t)):
                        dve.tensor_tensor(dst[:], ps_qkv[par][:, col:col + P].rearrange("p (a d) -> p a d", a=2)
                                          .unsqueeze(2).to_broadcast([P, 2, 2, C]), table, ALU.mult).then_inc(s_ropem, 1)
                t, par = s - LAG_MAX, (j - LAG_MAX) % 2
                if ok(t):
                    after(dve, s_score, t, 0)
                    sc = ps_score[par][:, :].rearrange("p (h k) -> p h k", k=N)
                    dve.reduce_max(smax[:, par, :], sc, AX).then_inc(s_max, 1)
                t, par = s - LAG_ROPE, (j - LAG_ROPE) % 2
                if ok(t):
                    after(dve, s_ropem, t, 0, 2)
                    after(dve, s_turn, t, 2)
                    dve.tensor_tensor(qk_bd[:, par, :, :, :], rope_c[:], rope_s[:], ALU.add).then_inc(s_qkbd, 1)
                t, par = s - LAG_MAX, (j - LAG_MAX) % 2
                if ok(t):
                    after(dve, s_max, t, 0)
                    after(dve, s_pt, t, 2)
                    dve.tensor_tensor(probs[:, par, :, :], sc, smax[:, par, :].unsqueeze(2).to_broadcast([P, HEADS, N]), ALU.subtract).then_inc(s_sub, 1)
                t, par = s - LAG_PROJ, (j - LAG_PROJ) % 2
                if ok(t):
                    after(dve, s_proj, t, 0)
                    dve.tensor_tensor(res_all[:, t, :], ps_proj, res_all[:, t, :], ALU.add).then_inc(s_t, 1)

            norm1_sums(0)
            norm1_scale(0)

            def body(b, ok, masked):
                if isinstance(b, int) and b == FIRST_TILES - 2 * G:
                    dve.wait_ge(x_in[1], 32)
                for j in range(G):
                    step(b, j, ok)
                    wt = split_group(b, masked)
                    if j == 0 and ok(b - 4 * G):
                        find_slots(b - 4 * G)
                    if j == 1 and ok(b - 4 * G):
                        weigh(b - 4 * G)
                    if j == 0 and ok(b - 3 * G):
                        norm2_scale(b - 3 * G)
                    if j == 0 and ok(b + G):
                        norm1_sums(b + G)
                    if j == 1 and wt is not None:
                        dve.wait_ge(s_whi, wt + G)
                        dve.tensor_tensor(wraw[:], wraw[:], wsp_part(wt, 0), ALU.subtract).then_inc(s_wrest, G)
                    if j == 2 and ok(b + G):
                        norm1_scale(b + G)
                    if j == 2 and wt is not None:
                        dve.wait_ge(s_wmid, wt + G)
                        dve.tensor_tensor(wsp_part(wt, 2), wraw[:], wsp_part(wt, 1), ALU.subtract).then_inc(s_wlo, G)
                    if j == 3 and ok(b - 2 * G):
                        norm2_sums(b - 2 * G)
                    if j == 3 and ok(b - 3 * G):
                        pick(b - 3 * G)
            groups(dve, body)

            dve.wait_ge(s_before, TILES + 1)
            dve.tensor_copy(before[:, 0, :], before[:, G, :]).then_inc(s_before, 1)
            dve.wait_ge(s_cnt, 1)
            dve.tensor_copy(cnt_f[:], ps_cnt).then_inc(s_tstep, 1)
            dve.wait_ge(s_tstep, 1)
            dve.tensor_scalar(til_f[:], cnt_f[:], float(SLOTS - 1), None, ALU.add).then_inc(s_tstep, 1)
            dve.tensor_tensor(padrow_f[:], cnt_f[:], region_base, ALU.add).then_inc(s_tstep, 1)
            dve.wait_ge(s_tstep, 3)
            dve.tensor_copy(til_i[:], til_f[:]).then_inc(s_tstep, 1)
            dve.tensor_copy(padrow_i[:], padrow_f[:]).then_inc(s_tstep, 1)
            dve.wait_ge(s_tstep, 5)
            dve.tensor_scalar(til_s[:], til_i[:], 9, None, ALU.arith_shift_right).then_inc(s_tstep, 1)
            dve.wait_ge(s_tstep, 6)
            dve.tensor_copy(til_f[:], til_s[:]).then_inc(s_tstep, 1)
            dve.wait_ge(s_tstep, 7)
            dve.tensor_scalar(til_m[:], til_f[:], 1.0, None, ALU.max).then_inc(s_tstep, 1)
            dve.wait_ge(s_tstep, 8)
            dve.tensor_tensor_scan(ends_f[:], til_m[:], zero8[:], 0.0, ALU.add, ALU.add).then_inc(s_tstep, 1)
            dve.wait_ge(s_tstep, 9)
            dve.tensor_copy(ends_i[:], ends_f[:]).then_inc(s_tile, 1)
            dve.engine_nop().then_inc(s_hid, 2)
            dve.engine_nop().then_inc(s_x2, 1)
            dve.engine_nop().then_inc(s_yb, 1)
            dve.engine_nop().then_inc(s_yout, 1)
            dve.engine_nop().then_inc(s_nextmeta, 1)

            def copy_rows(n):
                dve.wait_ge(s_x2, n + 2)
                dve.tensor_copy(xs[:, 1, :], ps_x[1][:, 0:SLOTS]).then_inc(s_xs, 1)

            def tail(k):
                dve.wait_ge(s_yt, k + 1)
                dve.wait_ge(s_tailmeta, k + 1)
                dve.wait_ge(s_yout, k + 1)
                y4 = ps_yt[:, :].rearrange("p (c h d) -> p c h d", h=2, d=C)
                gate = meta[:].bitcast(F32)[:, :, 0:1].to_broadcast([P, SUB, C])
                dve.tensor_tensor(y_a[:], y4[:, :, 0, :], gate, ALU.mult)
                dve.tensor_tensor(y_b[:], y4[:, :, 1, :], gate, ALU.mult).then_inc(s_yb, 1)

            copy_rows(0)
            start = 0
            for e in range(E):
                end = dve.value_load(ends_i[0:1, e:e + 1], min_val=e + 1, max_val=MAX_TILES)
                with dve.Fori(start, end) as n:
                    for c in range(CHUNKS):
                        q = n * CHUNKS + c
                        dve.wait_ge(s_silu, q + 1)
                        dve.wait_ge(s_yc, q + 1)
                        if c < FULL:
                            dve.tensor_tensor(hid[:, c % 3, :], gate_h[:, c % 2, :], ps_g[c % 2][:, :], ALU.mult).then_inc(s_hid, 1)
                        else:
                            dve.tensor_tensor(hid[0:C, c % 3, :], gate_h[0:C, c % 2, :], ps_h[c % 2][C:2 * C, :], ALU.mult).then_inc(s_hid, 1)
                        if c == 0:
                            tail(n)
                    copy_rows(n + 1)
                start = end
            tail(start)

        @block.gpsimd
        def _(pool):
            pool.memset(minus_half[:], -0.5).then_inc(s_half, 1)
            pool.wait_ge(c_in, 64)
            pool.wait_ge(x_in[0], 32)
            pool.wait_ge(init_s, 3)
            pool.wait_ge(s_half, 1)

            def center(x, mean, c, sq, s_mean, s_c, s_sq, s_var, s_norm, tg):
                after(pool, s_mean, tg, -(G - 1))
                after(pool, s_norm, tg, 1)
                pool.tensor_tensor(c[:], x, mean[:].unsqueeze(2).to_broadcast([P, G, C]), ALU.subtract).then_inc(s_c, G)
                after(pool, s_c, tg, -(G - 1))
                after(pool, s_var, tg, 1)
                pool.tensor_tensor(sq[:], c[:], c[:], ALU.mult).then_inc(s_sq, G)

            def scale1(tg, half):
                a = half * 2
                if half == 0:
                    after(pool, s1vare, tg, -(G - 1))
                    pool.tensor_tensor(ln1_rstd[:], ln1_vare[:], minus_half[:], ALU.pow).then_inc(s1rstd, G)
                after(pool, s1rstd, tg, -(G - 1))
                after(pool, s_xt, tg - G + a + 1, 0)
                pool.tensor_tensor(xn[:, a:a + 2, :], ln1_c[:, a:a + 2, :], ln1_rstd[:, a:a + 2].unsqueeze(2).to_broadcast([P, 2, C]), ALU.mult).then_inc(s1xn, 2)

            def scatter(tg, picks):
                for i in picks:
                    pool.indirect_dma_start(rows_dram, bass.IndirectOffsetOnAxis(ap=slot_u[:, i // 2, i % 2:i % 2 + 1], axis=0),
                                            rows[:, i // 2, i % 2, :], None).then_inc(s_scat, 16)

            def fill_meta(tg):
                after(pool, s_scat, tg, 1, 32)
                after(pool, s_gates, tg, -(G - 1))
                after(pool, s_slotf, tg, -(G - 1))
                hold(pool)
                m = rows[:, :, :, PARTS:ROW]
                pool.tensor_copy(m.bitcast(F32)[:, :, :, 0], gates[:])
                pool.tensor_copy(m[:, :, :, 1], tok_sb[:, tiles_of(tg)].unsqueeze(2).to_broadcast([P, G, 2])).then_inc(s_meta, G)
                pool.tensor_copy(slot_u[:], slot_f[:]).then_inc(s_slotu, G)
                after(pool, s_slotu, tg, -(G - 1))
                after(pool, s_meta, tg, -(G - 1))
                after(pool, s_rows, tg, -(G - 1))
                hold(pool)

            center(x_all[:, 0:G, :], ln1_mean, ln1_c, ln1_sq, s1mean, s1c, s1sq, s1var, s1xn, 0)
            scale1(0, 0)
            scale1(0, 1)

            def body(b, ok, masked):
                if isinstance(b, int) and b == FIRST_TILES - 2 * G:
                    pool.wait_ge(x_in[1], 32)
                for j in range(G):
                    tg = b - 3 * G
                    if j == 0 and ok(tg):
                        after(pool, s2vare, tg, -(G - 1))
                        pool.tensor_tensor(ln2_rstd[:], ln2_vare[:], minus_half[:], ALU.pow).then_inc(s2rstd, G)
                        after(pool, s2rstd, tg, -(G - 1))
                        after(pool, s_x2t, tg, 1)
                        after(pool, s_rest, tg, 1)
                        pool.tensor_tensor(xn2[:], ln2_c[:], ln2_rstd[:].unsqueeze(2).to_broadcast([P, G, C]), ALU.mult).then_inc(s2xn, G)
                    if j == 2 and ok(tg):
                        after(pool, s_hi, tg, -(G - 1))
                        after(pool, s_lo, tg, 1)
                        pool.tensor_tensor(split_r[:], xn2[:], parts[:, :, 1, :], ALU.subtract).then_inc(s_rest, G)
                    if j == 3 and ok(tg):
                        after(pool, s_mid, tg, -(G - 1))
                        pool.tensor_tensor(parts[:, :, 2, :], split_r[:], parts[:, :, 0, :], ALU.subtract).then_inc(s_lo, G)
                    tg = b + G
                    if j == 1 and ok(tg):
                        center(x_all[:, tiles_of(tg), :], ln1_mean, ln1_c, ln1_sq, s1mean, s1c, s1sq, s1var, s1xn, tg)
                    if j == 2 and ok(tg):
                        scale1(tg, 0)
                    if j == 3 and ok(tg):
                        scale1(tg, 1)
                    tg = b - 2 * G
                    if j == 3 and ok(tg):
                        center(res_all[:, tiles_of(tg), :], ln2_mean, ln2_c, ln2_sq, s2mean, s2c, s2sq, s2var, s2xn, tg)
                    tg = b - 4 * G
                    if j == 1 and ok(tg):
                        fill_meta(tg)
                    if j >= 1 and ok(tg):
                        scatter(tg, ((), (0, 1), (2, 3, 4), (5, 6, 7))[j])
            groups(pool, body)
            pool.engine_nop().then_inc(s_yc, 3)

            def add_rows(k):
                pool.wait_ge(s_yb, k + 2)
                pool.tensor_tensor(y_out[:], y_a[:], y_b[:], ALU.add).then_inc(s_yout, 1)
                pool.wait_ge(s_yout, k + 2)
                hold(pool)
                for c in range(SUB):
                    pool.indirect_dma_start(out, bass.IndirectOffsetOnAxis(ap=meta[:, c, 1:2], axis=0),
                                            y_out[:, c, :], None, compute_op=ALU.add).then_inc(s_added, 16)
                pool.wait_ge(s_added, (k + 1) * (16 * SUB))
                hold(pool)

            def keep_meta(n):
                pool.wait_ge(s_xin, (n + 1) * 16)
                pool.wait_ge(s_tailmeta, n + 1)
                hold(pool)
                pool.tensor_copy(meta_next[:], xin[:, :, PARTS:ROW]).then_inc(s_nextmeta, 1)

            pool.tensor_copy(meta[:], pad_sb[:, :, PARTS:ROW]).then_inc(s_tailmeta, 1)
            pool.wait_ge(s_tout, 16 * GROUPS)
            pool.wait_ge(s_dummy, 16)
            keep_meta(0)
            pool.wait_ge(s_tile, 2)
            start = 0
            for e in range(E):
                end = pool.value_load(ends_i[0:1, e:e + 1], min_val=e + 1, max_val=MAX_TILES)
                with pool.Fori(start, end) as n:
                    add_rows(n)
                    pool.wait_ge(s_nextmeta, n + 2)
                    hold(pool)
                    pool.tensor_copy(meta[:], meta_next[:]).then_inc(s_tailmeta, 1)
                    keep_meta(n + 1)
                start = end
            add_rows(start)


def window_order():
    n_side = SIDE // (WIN * DIL)
    wins, masked = [], []
    for img in range(BATCH):
        for w in range(PER_IMAGE):
            (masked if w >= PER_IMAGE - MASKED_PER_IMAGE else wins).append((img, w))
    src, dst = [], []
    for img, w in wins + masked:
        block, d = divmod(w, DIL * DIL)
        bh, bw = divmod(block, n_side)
        dh, dw = divmod(d, DIL)
        base = (img * PER_IMAGE + w) * N
        for n in range(N):
            i, j = divmod(n, WIN)
            row = (bh * WIN * DIL + i * DIL + dh + SHIFT) % SIDE
            col = (bw * WIN * DIL + j * DIL + dw + SHIFT) % SIDE
            src.append(base + n)
            dst.append((img * SIDE + row) * SIDE + col)
    return np.array(src), np.array(dst)


def constants():
    kf = np.zeros((P, K_COLS), np.float32)
    kf[:, K_IDENT:K_IDENT + P] = np.eye(P)
    half = HD // 4
    inv = (1.0 / 10000.0 ** (np.arange(half, dtype=np.float32) / half)).astype(np.float32)
    tok = np.arange(P) % N
    for ax, pos in enumerate((tok // WIN, tok % WIN)):
        ang = pos[:, None].astype(np.float32) * inv
        for hh in range(2):
            for d in range(half):
                for head in range(HEADS):
                    col = head * HD + ax * (HD // 2) + hh * half + d
                    for which, scale in enumerate((HD ** -0.5, 1.0)):
                        own = np.arange(P), which * 2 * C + (np.arange(P) // N) * C + col
                        kf[own[0], K_COS + own[1]] = np.cos(ang[:, d]) * scale
                        kf[own[0], K_SIN + own[1]] = np.sin(ang[:, d]) * scale * (1, -1)[hh == 0]
    kf[np.arange(P), K_PAIR + np.arange(P) % N] = 1
    kf[np.arange(P), K_HEADMASK + (np.arange(P) % C) // HD] = 1
    kf[np.arange(P), K_VMASK + np.arange(P) // N] = 1
    kf[:, K_IOTA:K_IOTA + E] = np.arange(E)
    kf[:, K_BASE:K_BASE + E] = np.arange(E) * REGION
    kb = np.zeros((P, B_COLS), np.float32)
    kb[:, B_IDENT:B_IDENT + P] = np.eye(P)
    kb[:, B_TRI:B_TRI + P] = np.arange(P)[:, None] < np.arange(P)[None, :]
    kb[:, B_ONES:B_ONES + P] = 1
    region = np.digitize(np.arange(N) // WIN, (WIN // 2, WIN // 2 + SHIFT // DIL))
    kb[:, B_MASK:B_MASK + N] = np.where(region[tok][:, None] != region[None, :], BIG, 0)
    tok_id = (np.arange(TILES)[None, :] * P + np.arange(P)[:, None]).astype(np.uint32)
    pad = np.zeros((P, SUB, ROW), np.uint32)
    pad[:, :, ROW - 1] = TOKENS + np.arange(SUB)[None, :] * P + np.arange(P)[:, None]
    return kf, (kb.view(np.uint32) >> 16).astype(np.uint16), tok_id, pad


def kernel(x, L0_conv_W_qkv, L0_conv_b_qkv, L0_conv_W_proj, L0_conv_b_proj, L0_ffn_router_w, L0_ffn_w1, L0_ffn_w2, L0_ffn_w3):
    import concourse.bacc as bacc
    from concourse.bass_utils import run_bass_kernel_spmd

    x = np.asarray(x)
    src, dst = window_order()
    flat = x.reshape(TOKENS, C)
    w1, w2, w3 = (np.asarray(a) for a in (L0_ffn_w1, L0_ffn_w2, L0_ffn_w3))
    w13 = np.zeros((E, C, WCOLS), np.float32)
    for c in range(FULL):
        w13[:, :, 2 * c * P:(2 * c + 1) * P] = w1[:, c * P:(c + 1) * P, :].transpose(0, 2, 1)
        w13[:, :, (2 * c + 1) * P:(2 * c + 2) * P] = w3[:, c * P:(c + 1) * P, :].transpose(0, 2, 1)
    w13[:, :, 2 * FULL * P:2 * FULL * P + REST] = w1[:, FULL * P:, :].transpose(0, 2, 1)
    w13[:, :, 2 * FULL * P + C:2 * FULL * P + C + REST] = w3[:, FULL * P:, :].transpose(0, 2, 1)
    w2t = np.zeros((P, E, CHUNKS, C), np.float32)
    for c in range(CHUNKS):
        k = min(P, H - c * P)
        w2t[0:k, :, c, :] = w2[:, :, c * P:c * P + k].transpose(2, 0, 1)
    router = np.zeros((P, 2 * E), np.float32)
    router[0:C, 0:E] = np.asarray(L0_ffn_router_w).T
    router[C:2 * C, E:2 * E] = np.asarray(L0_ffn_router_w).T
    kf, kb, tok_id, pad = constants()
    arrays = {
        "x_win": flat[src].reshape(TILES, P, C).transpose(1, 0, 2).copy(), "x_res": flat[dst].reshape(TILES, P, C).transpose(1, 0, 2).copy(),
        "w_qkv": np.concatenate([np.asarray(L0_conv_W_qkv), np.asarray(L0_conv_b_qkv)[None, :]], 0),
        "w_proj": np.concatenate([np.asarray(L0_conv_W_proj), np.asarray(L0_conv_b_proj)[None, :]], 0),
        "router": router, "w13": w13, "w2": w2t, "kf": kf, "kb": kb, "tok_id": tok_id, "pad_rows": pad,
    }
    nc = bacc.Bacc("TRN2", target_bir_lowering=False, num_devices=1)
    args = {n: nc.dram_tensor(n, a.shape, mybir.dt.from_np(a.dtype), kind="ExternalInput").ap() for n, a in arrays.items()}
    out = nc.dram_tensor("out", (TOKENS + SLOTS, C), F32, kind="ExternalOutput").ap()
    build(nc, out=out, **args)
    r = run_bass_kernel_spmd(nc, [arrays], core_ids=[0])
    rows = np.asarray(r.results[0]["out"])
    y = np.empty((TOKENS, C), np.float32)
    y[dst] = rows[0:TOKENS]
    return y.reshape(x.shape)
```

```python
from contextlib import ExitStack

import numpy as np

import concourse.bass as bass
from concourse import mybir

F32 = mybir.dt.float32
BF16 = mybir.dt.bfloat16
U32 = mybir.dt.uint32
U16 = mybir.dt.uint16
I32 = mybir.dt.int32
ALU = mybir.AluOpType
ACT = mybir.ActivationFunctionType
AX = mybir.AxisListType.X

P = 128
BATCH, SIDE, C = 4, 48, 64
HEADS, HD = 8, 8
WIN, DIL, SHIFT = 8, 2, 4
N = WIN * WIN
TOKENS = BATCH * SIDE * SIDE
TILES = TOKENS // P
PER_IMAGE = SIDE * SIDE // N
G = 4
GROUPS = TILES // G
QKV = 3 * C
E, H = 8, 682
FULL = H // P
REST = H - FULL * P
CHUNKS = FULL + 1
assert CHUNKS == 6
HALF_BLOCKS = (2 * FULL + 2) // 2
WHALF = HALF_BLOCKS * P
SLOTS = 384
SUB = SLOTS // P
REGION = TOKENS + SLOTS
MAX_TILES = 2 * TOKENS // SLOTS + E
PARTS = 3 * C // 2
ROW = PARTS + 2
EPS_C, EPS_T = 1e-6, 1e-5
BIG = -1.0e30
THIRD, THIRD_SHIFT = 171, 9
assert SUB == 3 and all(x * THIRD >> THIRD_SHIFT == x // SUB for x in range(TOKENS // P + SUB + 1))
MASKED_PER_IMAGE = PER_IMAGE // 3
MASK_TILE = BATCH * (PER_IMAGE - MASKED_PER_IMAGE) // 2
LAG_QKV, LAG_ROPE, LAG_TURN, LAG_KBD, LAG_V, LAG_SCORE, LAG_MAX, LAG_PT, LAG_PV, LAG_OT, LAG_PROJ = 1, 2, 2, 3, 3, 4, 5, 6, 7, 8, 8
FILL_GROUPS = 5
DRAIN_GROUPS = 4
LAST_SPLIT = FILL_GROUPS + E - 1
assert (LAST_SPLIT + 1) * G == MASK_TILE + LAG_SCORE
FIRST_TILES = 5 * G

K_IDENT, K_COS, K_SIN, K_PAIR, K_HEADMASK, K_VMASK, K_IOTA, K_BASE = 0, 128, 256, 384, 448, 456, 458, 466
K_COLS = 474
B_IDENT, B_TRI, B_ONES, B_MASK = 0, 128, 256, 384
B_COLS = 448


def build(nc, x_win, x_res, w_qkv, w_proj, router, w13, w2, kf, kb, tok_id, pad_rows, out):
    ctx = ExitStack()
    with ctx:
        def sb(name, shape, dt=F32):
            return ctx.enter_context(nc.sbuf_tensor(name, shape, dt))

        def sem(name):
            return ctx.enter_context(nc.semaphore(name))

        rows_dram = nc.dram_tensor("expert_rows", (E * REGION, ROW), U32, kind="Internal").ap()

        x_all = sb("x_all", [P, TILES, C])
        res_all = sb("res_all", [P, TILES, C])
        wqkv_sb = sb("wqkv_sb", [C + 1, QKV])
        wext = sb("wext", [C + 1, 2 * P + C])
        wproj_sb = sb("wproj_sb", [C + 1, C])
        router_sb = sb("router_sb", [P, 2 * E])
        w2_sb = sb("w2_sb", [P, E, CHUNKS, C])
        consts = sb("consts", [P, K_COLS])
        constb = sb("constb", [P, B_COLS], BF16)
        tok_sb = sb("tok_sb", [P, TILES], U32)
        pad_sb = sb("pad_sb", [P, SUB, ROW], U32)
        ident = consts[:, K_IDENT:K_IDENT + P]
        cos_sin = consts[:, K_COS:K_COS + 2 * P]
        pair = consts[:, K_PAIR:K_PAIR + N]
        head_mask = consts[:, K_HEADMASK:K_HEADMASK + HEADS]
        v_mask = consts[:, K_VMASK:K_VMASK + 2]
        iota8 = consts[:, K_IOTA:K_IOTA + E]
        region_base = consts[:, K_BASE:K_BASE + E]
        ident_b = constb[:, B_IDENT:B_IDENT + P]
        tri_b = constb[:, B_TRI:B_TRI + P]
        ones_b = constb[:, B_ONES:B_ONES + P]
        mask_b = constb[:, B_MASK:B_MASK + N]
        ln1_sum = sb("ln1_sum", [P, G])
        ln1_mean = sb("ln1_mean", [P, G])
        ln1_c = sb("ln1_c", [P, G, C])
        ln1_sq = sb("ln1_sq", [P, G, C])
        ln1_var = sb("ln1_var", [P, G])
        ln1_vare = sb("ln1_vare", [P, G])
        ln1_rstd = sb("ln1_rstd", [P, G])
        xn = sb("xn", [P, G, C])
        xt = sb("xt", [C + 1, 2, 4, N])
        rope = sb("rope", [P, 2, 2, C])
        qk_bd = sb("qk_bd", [P, 2, 2, 2, C])
        qkt = sb("qkt", [P, 2, P + N])
        k_bd = sb("k_bd", [P, 2, HEADS, N])
        v_bd = sb("v_bd", [P, G, 2, 4, 18])
        smax = sb("smax", [P, 2, HEADS])
        probs = sb("probs", [P, 2, HEADS, N])
        pt = sb("pt", [P, 2, 4, P])
        rden = sb("rden", [P, 2, HEADS])
        att = sb("att", [P, 2, C])
        att_t = sb("att_t", [C + 1, 2, P])
        ln2_sum = sb("ln2_sum", [P, G])
        ln2_mean = sb("ln2_mean", [P, G])
        ln2_c = sb("ln2_c", [P, G, C])
        ln2_sq = sb("ln2_sq", [P, G, C])
        ln2_var = sb("ln2_var", [P, G])
        ln2_vare = sb("ln2_vare", [P, G])
        ln2_rstd = sb("ln2_rstd", [P, G])
        xn2 = sb("xn2", [P, G, C])
        xn2_t = sb("xn2_t", [P, 2, P])
        split_r = sb("split_r", [P, G, C])
        parts = sb("parts", [P, G, 3, C], BF16)
        rows = sb("rows", [P, G, 2, ROW], U32)
        logits = sb("logits", [P, G, E])
        top = sb("top", [P, G, E])
        top_i = sb("top_i", [P, G, E], U32)
        top_if = sb("top_if", [P, G, 2])
        top_d = sb("top_d", [P, G, E])
        top_e = sb("top_e", [P, G, E])
        zsum = sb("zsum", [P, G])
        two = sb("two", [P, G])
        gden = sb("gden", [P, G])
        grec = sb("grec", [P, G])
        gates = sb("gates", [P, G, 2])
        chosen = sb("chosen", [P, G, 2, E])
        members = sb("members", [P, G, E], BF16)
        counted = sb("counted", [P, E], BF16)
        group_sum = sb("group_sum", [P, E])
        place = sb("place", [P, G, E])
        place2 = sb("place2", [P, G, 2, E])
        slot_f = sb("slot_f", [P, G, 2])
        slot_u = sb("slot_u", [P, G, 2], U32)
        cnt_f = sb("cnt_f", [P, E])
        cnt_i = sb("cnt_i", [P, E], I32)
        til_i = sb("til_i", [P, E], I32)
        til_s = sb("til_s", [P, E], I32)
        til_f = sb("til_f", [P, E])
        til_m = sb("til_m", [P, E])
        ends_f = sb("ends_f", [P, E])
        zero8 = sb("zero8", [P, E])
        minus_half = sb("minus_half", [P, G])
        ends_i = sb("ends_i", [P, E], I32)
        padrow_f = sb("padrow_f", [P, E])
        padrow_i = sb("padrow_i", [P, E], I32)
        wraw = sb("wraw", [P, WHALF])
        wparts = sb("wparts", [P, 3, WHALF], BF16)
        wsp = sb("wsp", [P, E, 2, 3, WHALF], BF16)
        xin = sb("xin", [P, SUB, ROW], U32)
        meta = sb("meta", [P, SUB, 2], U32)
        meta_next = sb("meta_next", [P, SUB, 2], U32)
        xs = sb("xs", [P, 2, SLOTS], BF16)
        gate_h = sb("gate_h", [P, 2, SLOTS])
        hid = sb("hid", [P, 3, SLOTS])
        y_t = sb("y_t", [P, SLOTS])
        y_a = sb("y_a", [P, SUB, C])
        y_b = sb("y_b", [P, SUB, C])
        y_out = sb("y_out", [P, SUB, C])

        ps = [ctx.enter_context(nc.psum_tensor(f"bank{i}", [P, 512], F32)) for i in range(8)]
        ps_xt = ps[0][0:C, 0:P]
        ps_ot = ps[0][0:C, P:2 * P]
        ps_xn2t = ps[0][:, 2 * P:4 * P]
        ps_log = ps[0][:, 0:G * E]
        ps_qkv = [ps[1], ps[2]]
        ps_pos = ps[1][:, QKV + C + 2 * C:QKV + C + 2 * C + G * E]
        ps_turn = ps[3][:, 0:P + N]
        ps_score = [ps[4], ps[5]]
        ps_pt = ps[6]
        ps_pv = ps[7][:, 0:72]
        ps_proj = ps[7][:, 128:128 + C]
        ps_cnt = ps[7][:, 320:320 + E]
        ps_x = [ps[0][:, :].bitcast(BF16), ps[7][:, :].bitcast(BF16)]
        ps_h = [ps[1][:, 0:SLOTS], ps[2][:, 0:SLOTS]]
        ps_g = [ps[3][:, 0:SLOTS], ps[4][:, 0:SLOTS]]
        ps_y = ps[5][:, 0:SLOTS]
        ps_yt = ps[6][:, 0:SLOTS]

        c_in, cb_in = sem("float_consts_in"), sem("other_consts_in")
        x_in, res_in, rest_in = sem("first_x_in"), sem("first_residual_in"), sem("rest_in")
        s_half = sem("minus_half_set")
        s_dummy = sem("dummy_rows_stored")
        w_in, wr_in, w2_in = sem("w_qkv_in"), sem("w_proj_and_router_in"), sem("w2_in")
        init_s = sem("init_done")
        wext_s = sem("wext_done")
        s1sum, s1mean, s1c, s1sq, s1var, s1vare, s1rstd, s1xn = [sem("ln1_" + n) for n in ("sum", "mean", "c", "sq", "var", "vare", "rstd", "xn")]
        s_xt, s_xtc = sem("xt_ps"), sem("xt_sb")
        s_qkv, s_ropem, s_qkbd, s_vbd = sem("qkv_ps"), sem("rope_mul"), sem("qk_bd_done"), sem("v_bd_done")
        s_turn, s_qktc, s_kbd = sem("turn_ps"), sem("qkt_sb"), sem("k_bd_done")
        s_score, s_max, s_sub, s_exp = sem("score_ps"), sem("max_done"), sem("sub_done"), sem("exp_done")
        s_pt, s_ptc = sem("pt_ps"), sem("pt_sb")
        s_pv, s_rden, s_att = sem("pv_ps"), sem("rden_done"), sem("att_done")
        s_ot, s_otc = sem("ot_ps"), sem("ot_sb")
        s_proj, s_t = sem("proj_ps"), sem("t_done")
        s_tout = sem("t_stored")
        s2sum, s2mean, s2c, s2sq, s2var, s2vare, s2rstd, s2xn = [sem("ln2_" + n) for n in ("sum", "mean", "c", "sq", "var", "vare", "rstd", "xn")]
        s_x2t, s_x2tc, s_log, s_logc = sem("xn2t_ps"), sem("xn2t_sb"), sem("logits_ps"), sem("logits_sb")
        s_hi, s_rest, s_mid, s_lo = sem("high_part"), sem("rest_of_high"), sem("middle_part"), sem("low_part")
        s_max8, s_idx, s_idxf, s_topd, s_tope = sem("max8"), sem("idx8"), sem("idx_f"), sem("top_d"), sem("top_e")
        s_z, s_gden, s_grec, s_gates = sem("z_two"), sem("gate_den"), sem("gate_rec"), sem("gates_done")
        s_chosen, s_members, s_gsum, s_counted, s_tstep = sem("chosen_done"), sem("members_done"), sem("group_sum"), sem("counted_done"), sem("tile_count_step")
        s_pos, s_place, s_place2, s_slotf, s_slotu = sem("pos_ps"), sem("place"), sem("place2"), sem("slot_f"), sem("slot_u")
        s_rows, s_meta = sem("rows_done"), sem("rows_meta")
        s_scat = sem("rows_scattered")
        s_pad = sem("pads_stored")
        s_cnt, s_tile = sem("count_ps"), sem("tile_counts")
        s_wraw, s_wstack, s_wfree = sem("wraw_in"), sem("w_stacked"), sem("wparts_free")
        s_whi, s_wrest, s_wmid, s_wlo = sem("w_high"), sem("w_rest_of_high"), sem("w_middle"), sem("w_low")
        s_xin, s_x2, s_xs = sem("xin_in"), sem("x_ps"), [sem("xs_middle_high_sb"), sem("xs_high_low_sb")]
        s_h, s_g, s_silu, s_hid, s_yc = sem("h_ps"), sem("g_ps"), sem("silu_done"), sem("hid_done"), sem("y_chunk")
        s_ytsb, s_yt = sem("yt_sb"), sem("yt_ps")
        s_yb, s_yout, s_added = sem("y_b"), sem("y_out_done"), sem("y_added")
        s_tailmeta, s_nextmeta = sem("tail_meta"), sem("next_meta")

        w13_rows = w13.rearrange("e p f -> (e p) f")
        wsp_flat = wsp[:].rearrange("p e h i f -> p (e h i f)")
        out_v = out[0:TOKENS, :].rearrange("(t p) c -> p t c", p=P)

        block = ctx.enter_context(nc.Block())

        def groups(eng, body):
            def ok(t):
                return not isinstance(t, int) or 0 <= t < TILES
            for g in range(FILL_GROUPS):
                body(g * G, ok, False)
            with eng.Fori(FILL_GROUPS * G, LAST_SPLIT * G, G) as b:
                body(b, ok, False)
            body(LAST_SPLIT * G, ok, False)
            with eng.Fori((LAST_SPLIT + 1) * G, TILES - G, G) as b:
                body(b, ok, True)
            for g in range(GROUPS - 1, GROUPS + DRAIN_GROUPS):
                body(g * G, ok, True)

        def tiles_of(tg):
            if isinstance(tg, int):
                return bass.ds(tg, G)
            return bass.ds(nc.s_assert_within(tg, 0, TILES - G, skip_runtime_bounds_check_because="the loops step through whole groups"), G)

        def split_group(b, masked):
            if not masked and (not isinstance(b, int) or b == LAST_SPLIT * G):
                return b - FILL_GROUPS * G
            return None

        def within(v, last):
            if isinstance(v, int):
                return v
            return nc.s_assert_within(v, 0, last, skip_runtime_bounds_check_because="the first loop has a group for every expert but the last")

        def after(eng, s, t, back, scale=1):
            v = (t - back + 1) * scale if scale != 1 else t - back + 1
            if not isinstance(v, int):
                eng.wait_ge(s, v)
            elif v > 0:
                eng.wait_ge(s, min(v, TILES * scale))

        def hold(eng):
            eng.nop(nofuse=True)

        @block.sync
        def _(sp):
            sp.dma_start(x_all[:, 0:FIRST_TILES, :], x_win[:, 0:FIRST_TILES, :]).then_inc(x_in, 16)
            sp.dma_start(consts[:], kf).then_inc(c_in, 16)
            sp.dma_start(wqkv_sb[:], w_qkv).then_inc(w_in, 16)
            for dst, src in ((constb[:].bitcast(U16), kb), (tok_sb[:], tok_id), (pad_sb[:], pad_rows)):
                sp.dma_start(dst, src).then_inc(cb_in, 16)
            for dst, src in ((wproj_sb[:], w_proj), (router_sb[:], router)):
                sp.dma_start(dst, src).then_inc(wr_in, 16)
            sp.dma_start(res_all[:, 0:FIRST_TILES, :], x_res[:, 0:FIRST_TILES, :]).then_inc(res_in, 16)
            sp.dma_start(x_all[:, FIRST_TILES:, :], x_win[:, FIRST_TILES:, :]).then_inc(rest_in, 16)
            sp.dma_start(res_all[:, FIRST_TILES:, :], x_res[:, FIRST_TILES:, :]).then_inc(rest_in, 16)
            sp.dma_start(w2_sb[:], w2).then_inc(w2_in, 16)
            sp.dma_start(wraw[:], w13[0]).then_inc(s_wraw, 16)
            sp.wait_ge(x_in, 16)
            sp.dma_start(out[TOKENS:TOKENS + SLOTS, :].rearrange("(c p) d -> p c d", p=P), x_all[:, 0:SUB, :]).then_inc(s_dummy, 16)

            sp.nop(nofuse=True).then_inc(s_wfree, G)

            def body(b, ok, masked):
                wt = split_group(b, masked)
                if wt is not None:
                    sp.wait_ge(s_wlo, wt + G)
                    for half in range(2):
                        src = wparts[half * C:(half + 1) * C, :, :]
                        at = within(wt * (2 * 3 * WHALF // G) + half * 3 * WHALF, E * 2 * 3 * WHALF - 3 * WHALF)
                        lower = wsp_flat[C:2 * C, bass.ds(at, 3 * WHALF)].rearrange("p (i f) -> p i f", i=3)
                        sp.dma_start(wsp_flat[0:C, bass.ds(at, 3 * WHALF)], src.rearrange("p i f -> p (i f)")).then_inc(s_wstack, 16)
                        sp.dma_start(lower[:, 0:1, :], src[:, 1:2, :]).then_inc(s_wstack, 16)
                        sp.dma_start(lower[:, 1:3, :], src[:, 0:1, :].to_broadcast([C, 2, WHALF])).then_inc(s_wstack, 16)
                    if not isinstance(b, int):
                        row = within(wt * (P // G) + P, (E - 1) * P)
                        sp.dma_start(wraw[:], w13_rows[bass.ds(row, P), :]).then_inc(s_wraw, 16)
                        sp.wait_ge(s_wstack, wt * (6 * 16 // G) + 6 * 16)
                        sp.nop(nofuse=True).then_inc(s_wfree, G)
                tg = b - 2 * G
                if ok(tg):
                    after(sp, s_t, tg, -(G - 1))
                    sp.dma_start(out_v[:, tiles_of(tg), :], res_all[:, tiles_of(tg), :]).then_inc(s_tout, 16)
            groups(sp, body)

            sp.wait_ge(s_tile, 2)
            for e in range(E):
                at = sp.value_load(padrow_i[0:1, e:e + 1], min_val=e * REGION, max_val=e * REGION + TOKENS)
                sp.dma_start(rows_dram[bass.ds(at, SLOTS), :].rearrange("(c p) r -> p c r", p=P),
                             pad_sb[:]).then_inc(s_pad, 16)
            sp.wait_ge(s_pad, 16 * E)
            sp.wait_ge(s_scat, 16 * 2 * TILES)
            start = 0
            for e in range(E):
                end = sp.value_load(ends_i[0:1, e:e + 1], min_val=e + 1, max_val=MAX_TILES)
                with sp.Fori(start, end) as n:
                    row0 = nc.s_assert_within((n - start) * SLOTS + e * REGION, e * REGION, e * REGION + TOKENS,
                                              skip_runtime_bounds_check_because="an expert's tiles hold at most all tokens")
                    sp.wait_ge(s_x2, n + 1)
                    sp.wait_ge(s_nextmeta, n + 1)
                    sp.dma_start(xin[:], rows_dram[bass.ds(row0, SLOTS), :].rearrange("(c p) r -> p c r", p=P)).then_inc(s_xin, 16)
                start = end
            sp.wait_ge(s_x2, start + 1)
            sp.wait_ge(s_nextmeta, start + 1)
            sp.dma_start(xin[:], pad_sb[:]).then_inc(s_xin, 16)
            sp.wait_ge(s_tout, 16 * GROUPS)
            sp.wait_ge(s_dummy, 16)
            sp.wait_ge(s_added, (start + 1) * (16 * SUB))
            hold(sp)

        @block.tensor
        def _(pe):
            pe.wait_ge(c_in, 16)
            pe.wait_ge(wext_s, 3)
            pe.wait_ge(w_in, 16)
            pe.wait_ge(init_s, 4)

            def step(b, j, ok, masked):
                s = b + j
                t, par = s - LAG_PV, (j - LAG_PV) % 2
                if ok(t):
                    after(pe, s_ptc, t, 0)
                    after(pe, s_vbd, t, 0)
                    after(pe, s_t, s - LAG_PROJ, 1)
                    after(pe, s_att, t, 1)
                    for pr in range(4):
                        for w in range(2):
                            mm = pe.matmul(ps_pv[w * N:(w + 1) * N, pr * 18:(pr + 1) * 18],
                                           pt[:, par, pr, w * N:(w + 1) * N],
                                           v_bd[:, (j - LAG_PV) % G, w, pr, :], start=True, stop=True)
                    mm.then_inc(s_pv, 1)
                t, par = s - LAG_PT, (j - LAG_PT) % 2
                if ok(t):
                    after(pe, s_exp, t, 0)
                    after(pe, s_ptc, t, 1)
                    for pr in range(4):
                        mm = pe.transpose(ps_pt[:, pr * P:(pr + 1) * P], probs[:, par, 2 * pr:2 * pr + 2, :], ident)
                    mm.then_inc(s_pt, 1)
                t, par = s - LAG_OT, (j - LAG_OT) % 2
                if ok(t):
                    after(pe, s_att, t, 0)
                    after(pe, s_xtc, s, 1)
                    if j == 2 and ok(b - 3 * G):
                        after(pe, s_x2tc, b - 3 * G, -(G - 1))
                    if j == 3 and ok(b - 3 * G):
                        after(pe, s_logc, b - 3 * G, -(G - 1))
                    hold(pe)
                    pe.transpose(ps_ot, att[:, par, :], ident).then_inc(s_ot, 1)
                t, par = s - LAG_SCORE, (j - LAG_SCORE) % 2
                if ok(t):
                    after(pe, s_qktc, t, 0)
                    after(pe, s_kbd, t, 0)
                    after(pe, s_sub, t, 2)
                    mm = pe.matmul(ps_score[par][:, :], qkt[:, par, 0:P], k_bd[:, par, :, :], start=True, stop=not masked)
                    if masked:
                        mm = pe.matmul(ps_score[par][:, :], ident_b, mask_b.unsqueeze(1).to_broadcast([P, HEADS, N]), start=False, stop=True)
                    mm.then_inc(s_score, 1)
                t, par = s - LAG_PROJ, (j - LAG_PROJ) % 2
                if ok(t):
                    after(pe, s_otc, t, 0)
                    after(pe, s_att, s - LAG_PV, 0)
                    after(pe, s_t, t, 1)
                    pe.matmul(ps_proj, att_t[:, par, :], wproj_sb[:], start=True, stop=True).then_inc(s_proj, 1)
                t, par = s - LAG_TURN, (j - LAG_TURN) % 2
                if ok(t):
                    after(pe, s_qkbd, t, 0)
                    after(pe, s_qktc, t, 1)
                    pe.transpose(ps_turn[:, 0:P], qk_bd[:, par, 0, :, :], ident)
                    pe.matmul(ps_turn[:, P:P + N], qk_bd[:, par, 1, :, :], pair, start=True, stop=True).then_inc(s_turn, 1)
                tg = b - 3 * G
                if j == 1 and ok(tg):
                    after(pe, s2xn, tg, -(G - 1))
                    after(pe, s_xtc, s, 1)
                    after(pe, s_otc, s - LAG_OT, 0)
                    for m in range(2):
                        mm = pe.transpose(ps_xn2t[:, m * P:(m + 1) * P], xn2[:, 2 * m:2 * m + 2, :], ident)
                    mm.then_inc(s_x2t, G)
                if j == 2 and ok(tg):
                    after(pe, s_x2tc, tg, -(G - 1))
                    after(pe, s_xtc, s, 1)
                    after(pe, s_otc, s - LAG_OT, 0)
                    for m in range(2):
                        mm = pe.matmul(ps_log[:, m * 2 * E:(m + 1) * 2 * E], xn2_t[:, m, :], router_sb[:], start=True, stop=True)
                    mm.then_inc(s_log, G)
                tg = b - 3 * G
                if j == G - 1 and ok(tg):
                    after(pe, s_members, tg, -(G - 1))
                    pe.wait_ge(s_counted, tg + G)
                    after(pe, s_ropem, s - LAG_QKV, 2)
                    after(pe, s_vbd, s - LAG_QKV, 2)
                    pe.matmul(ps_pos, tri_b, members[:], start=True, stop=False)
                    for g in range(1, G):
                        pe.matmul(ps_pos[:, g * E:G * E], ones_b, members[:, 0:G - g, :], start=False, stop=False)
                    pe.matmul(ps_pos, ones_b, counted[:].unsqueeze(1).to_broadcast([P, G, E]), start=False, stop=True).then_inc(s_pos, G)
                t, par = s - LAG_QKV, (j - LAG_QKV) % 2
                if ok(t):
                    after(pe, s_xtc, t, 0)
                    if j == 1 and ok(b - 4 * G):
                        after(pe, s_place, b - 4 * G, -(G - 1))
                    after(pe, s_ropem, t, 2)
                    after(pe, s_vbd, t, 2)
                    pe.matmul(ps_qkv[par][:, 0:2 * P], xt[:, par, 1:3, :], wext[:, 0:2 * P], start=True, stop=True)
                    for w in range(2):
                        mm = pe.matmul(ps_qkv[par][:, 2 * P + w * C:2 * P + (w + 1) * C],
                                       xt[:, par, 2 * w:2 * w + 2, :],
                                       wext[:, 2 * P:2 * P + C], start=True, stop=True)
                    mm.then_inc(s_qkv, 1)
                t, par = s, j % 2
                if ok(t):
                    after(pe, s1xn, t, 0)
                    after(pe, s_xtc, t, 1)
                    after(pe, s_otc, s - LAG_OT, 0)
                    if j == 1 and ok(b - 3 * G):
                        after(pe, s_x2tc, b - 3 * G, -(G - 1))
                    if j == 2 and ok(b - 3 * G):
                        after(pe, s_logc, b - 3 * G, -(G - 1))
                    hold(pe)
                    pe.transpose(ps_xt, xn[:, j, :], ident).then_inc(s_xt, 1)

            def body(b, ok, masked):
                if isinstance(b, int) and b == LAG_PROJ:
                    pe.wait_ge(wr_in, 32)
                    pe.wait_ge(cb_in, 48)
                for j in range(G):
                    step(b, j, ok, masked)
            groups(pe, body)

            pe.wait_ge(s_counted, TILES + G)
            after(pe, s_place, TILES - 1, 0)
            pe.matmul(ps_cnt, ones_b, counted[:], start=True, stop=True).then_inc(s_cnt, 1)

            def turn_rows(n):
                pe.wait_ge(s_xin, (n + 1) * 16)
                for k in range(2):
                    for c in range(SUB):
                        mm = pe.transpose(ps_x[k][:, c * P:(c + 1) * P], xin[:, c, 0:PARTS].bitcast(BF16)[:, k * C:(k + 2) * C], ident_b)
                mm.then_inc(s_x2, 1)

            def hidden(n, e, c):
                q = n * CHUNKS + c
                if c == 0:
                    pe.wait_ge(s_xs[0], n + 1)
                pe.wait_ge(s_hid, q + 1)
                for which in range(1 if c == FULL else 2):
                    dst = (ps_h, ps_g)[which][c % 2][:, :]
                    half, block = divmod(2 * c + which, HALF_BLOCKS)
                    for part in range(3):
                        if c == 0 and which == 0 and part == 2:
                            pe.wait_ge(s_xs[1], n + 1)
                        mm = pe.matmul(dst, wsp[:, e, half, part, block * P:(block + 1) * P], xs[:, part // 2, :],
                                       start=(part == 0), stop=(part == 2))
                    mm.then_inc((s_h, s_g)[which], 1)

            def down(n, e, c):
                pe.wait_ge(s_hid, n * CHUNKS + (c + 3))
                if c == 0:
                    pe.wait_ge(s_ytsb, n + 1)
                half = c % 2
                mm = pe.matmul(ps_y[half * C:(half + 1) * C, :], w2_sb[:, e, c, :], hid[:, c % 3, :],
                               start=(c < 2), stop=(c >= CHUNKS - 2))
                mm.then_inc(s_yc, 1)

            def turn_y(k):
                pe.wait_ge(s_ytsb, k + 1)
                pe.wait_ge(s_yb, k + 1)
                for c in range(SUB):
                    mm = pe.transpose(ps_yt[:, c * P:(c + 1) * P], y_t[:, c * P:(c + 1) * P], ident)
                mm.then_inc(s_yt, 1)

            pe.wait_ge(s_wstack, 6 * 16 * E)
            pe.wait_ge(w2_in, 16)
            turn_rows(0)
            start = 0
            for e in range(E):
                end = pe.value_load(ends_i[0:1, e:e + 1], min_val=e + 1, max_val=MAX_TILES)
                with pe.Fori(start, end) as n:
                    hidden(n, e, 0)
                    turn_y(n)
                    hidden(n, e, 1)
                    hidden(n, e, 2)
                    down(n, e, 0)
                    hidden(n, e, 3)
                    down(n, e, 1)
                    hidden(n, e, 4)
                    hidden(n, e, 5)
                    down(n, e, 2)
                    turn_rows(n + 1)
                    down(n, e, 3)
                    down(n, e, 4)
                    down(n, e, 5)
                start = end
            turn_y(start)

        @block.scalar
        def _(act):
            act.wait_ge(c_in, 16)
            act.wait_ge(init_s, 4)

            def step(b, j, ok, masked):
                s = b + j
                t, par = s - LAG_OT, (j - LAG_OT) % 2
                if ok(t):
                    after(act, s_ot, t, 0)
                    after(act, s_proj, t, 2)
                    act.activation(att_t[0:C, par, :], ps_ot, ACT.Copy).then_inc(s_otc, 1)
                t, par = s - LAG_PT, (j - LAG_PT) % 2
                if ok(t):
                    after(act, s_pt, t, 0)
                    after(act, s_pv, t, 2)
                    act.activation(pt[:, par, :, :], ps_pt[:, :], ACT.Copy).then_inc(s_ptc, 1)
                t, par = s - LAG_V, (j - LAG_V) % 2
                if ok(t):
                    after(act, s_qkv, t, 0)
                    after(act, s_ropem, t, 0)
                    if j == 1 and ok(b - 4 * G):
                        after(act, s_place, b - 4 * G, -(G - 1))
                    after(act, s_pv, t, 4)
                    v = ps_qkv[par][:, 2 * P:2 * P + 2 * C].rearrange("p (w a d) -> p w a d", w=2, d=2 * HD)
                    for h in range(2):
                        mm = act.activation(v_bd[:, (j - LAG_V) % G, :, :, h * HD:(h + 1) * HD], v[:, :, :, h * HD:(h + 1) * HD],
                                            ACT.Copy, scale=v_mask[:, h:h + 1])
                    mm.then_inc(s_vbd, 1)
                wt = split_group(b, masked)
                if j == 3 and wt is not None:
                    act.wait_ge(s_wrest, wt + G)
                    act.activation(wparts[:, 1, :], wraw[:], ACT.Copy).then_inc(s_wmid, G)
                t, par = s - LAG_TURN, (j - LAG_TURN) % 2
                if ok(t):
                    after(act, s_turn, t, 0)
                    after(act, s_score, t, 2)
                    after(act, s_kbd, t, 2)
                    act.activation(qkt[:, par, :], ps_turn, ACT.Copy).then_inc(s_qktc, 1)
                tg = b - 3 * G
                if j == 1 and ok(tg):
                    after(act, s_x2t, tg, -(G - 1))
                    act.activation(xn2_t[:].rearrange("p a d -> p (a d)"), ps_xn2t, ACT.Copy).then_inc(s_x2tc, G)
                if j == 2 and ok(tg):
                    after(act, s_log, tg, -(G - 1))
                    after(act, s_idx, tg, 1)
                    act.activation(logits[:].rearrange("p a d -> p (a d)"), ps_log, ACT.Copy).then_inc(s_logc, G)
                t, par = s - LAG_MAX, (j - LAG_MAX) % 2
                if ok(t):
                    after(act, s_sub, t, 0)
                    act.activation(probs[:, par, :, :], probs[:, par, :, :], ACT.Exp).then_inc(s_exp, 1)
                t, par = s, j % 2
                if ok(t):
                    after(act, s_xt, t, 0)
                    after(act, s_qkv, t, 2)
                    act.activation(xt[0:C, par, :, :].rearrange("p (w r) n -> p w r n", r=2),
                                   ps_xt.rearrange("p (w n) -> p w n", w=2).unsqueeze(2).to_broadcast([C, 2, 2, N]), ACT.Copy).then_inc(s_xtc, 1)

            def body(b, ok, masked):
                for j in range(G):
                    step(b, j, ok, masked)
                    tg = b - 4 * G
                    if j == 0 and ok(tg):
                        after(act, s_lo, tg, -(G - 1))
                        after(act, s_scat, tg, 1, 32)
                        for k in range(2):
                            mm = act.activation(rows[:, :, k, 0:PARTS].bitcast(BF16), parts[:].rearrange("p g i d -> p g (i d)"), ACT.Copy)
                        mm.then_inc(s_rows, G)
                    tg = b - 3 * G
                    if j == 1 and ok(tg):
                        after(act, s2xn, tg, -(G - 1))
                        after(act, s_rows, tg, 1)
                        act.activation(parts[:, :, 1, :], xn2[:], ACT.Copy).then_inc(s_hi, G)
                    if j == 2 and ok(tg):
                        after(act, s_rest, tg, -(G - 1))
                        act.activation(parts[:, :, 0, :], split_r[:], ACT.Copy).then_inc(s_mid, G)
                    if j == 3 and ok(tg):
                        after(act, s_topd, tg, -(G - 1))
                        after(act, s_z, tg, 1)
                        after(act, s_gates, tg, 1)
                        act.activation(top_e[:], top_d[:], ACT.Exp).then_inc(s_tope, G)
                    wt = split_group(b, masked)
                    if j == 1 and wt is not None:
                        act.wait_ge(s_wraw, wt * (16 // G) + 16)
                        act.wait_ge(s_wfree, wt + G)
                        act.activation(wparts[:, 0, :], wraw[:], ACT.Copy).then_inc(s_whi, G)
            groups(act, body)

            act.activation(gate_h[:, 0, 0:E], ident[:, 0:E], ACT.Silu)

            def copy_rows(n):
                act.wait_ge(s_x2, n + 2)
                act.activation(xs[:, 0, :], ps_x[0][:, 0:SLOTS], ACT.Copy).then_inc(s_xs[0], 1)

            copy_rows(0)
            start = 0
            for e in range(E):
                end = act.value_load(ends_i[0:1, e:e + 1], min_val=e + 1, max_val=MAX_TILES)
                with act.Fori(start, end) as n:
                    for c in range(CHUNKS):
                        q = n * CHUNKS + c
                        act.wait_ge(s_h, q + 1)
                        act.wait_ge(s_hid, q + 1)
                        rows_c = P if c < FULL else C
                        act.activation(gate_h[0:rows_c, c % 2, :], ps_h[c % 2][0:rows_c, :], ACT.Silu).then_inc(s_silu, 1)
                    copy_rows(n + 1)
                    act.wait_ge(s_yc, n * CHUNKS + (CHUNKS + 3))
                    act.wait_ge(s_yt, n + 1)
                    act.activation(y_t[:], ps_y[:, :], ACT.Copy).then_inc(s_ytsb, 1)
                start = end

        @block.vector
        def _(dve):
            dve.memset(xt[C:C + 1, :, :, :], 1.0).then_inc(init_s, 1)
            dve.memset(att_t[C:C + 1, :, :], 1.0).then_inc(init_s, 1)
            dve.memset(y_t[:], 0.0).then_inc(s_ytsb, 1)
            dve.memset(qk_bd[:], 0.0).then_inc(init_s, 1)
            dve.memset(zero8[:], 0.0).then_inc(s_tile, 1)
            dve.memset(counted[:], 0.0).then_inc(s_counted, G)
            def ln1_total(tg):
                after(dve, s1mean, tg, 1)
                dve.reduce_sum(ln1_sum[:], x_all[:, tiles_of(tg), :], AX).then_inc(s1sum, G)

            def ln1_average(tg):
                after(dve, s1sum, tg, -(G - 1))
                after(dve, s1c, tg, 1)
                dve.tensor_scalar(ln1_mean[:], ln1_sum[:], 1.0 / C, None, ALU.mult).then_inc(s1mean, G)

            def ln1_squares(tg):
                after(dve, s1sq, tg, -(G - 1))
                dve.reduce_sum(ln1_var[:], ln1_sq[:], AX).then_inc(s1var, G)

            def ln1_variance(tg):
                after(dve, s1var, tg, -(G - 1))
                after(dve, s1rstd, tg, 1)
                dve.tensor_scalar(ln1_vare[:], ln1_var[:], 1.0 / C, EPS_C, ALU.mult, ALU.add).then_inc(s1vare, G)

            def ln2_total(tg):
                after(dve, s_t, tg, -(G - 1))
                dve.reduce_sum(ln2_sum[:], res_all[:, tiles_of(tg), :], AX).then_inc(s2sum, G)

            def ln2_average(tg):
                after(dve, s2sum, tg, -(G - 1))
                after(dve, s2c, tg, 1)
                dve.tensor_scalar(ln2_mean[:], ln2_sum[:], 1.0 / C, None, ALU.mult).then_inc(s2mean, G)

            def ln2_squares(tg):
                after(dve, s2sq, tg, -(G - 1))
                dve.reduce_sum(ln2_var[:], ln2_sq[:], AX).then_inc(s2var, G)

            def ln2_variance(tg):
                after(dve, s2var, tg, -(G - 1))
                after(dve, s2rstd, tg, 1)
                dve.tensor_scalar(ln2_vare[:], ln2_var[:], 1.0 / C, EPS_T, ALU.mult, ALU.add).then_inc(s2vare, G)

            def pick(tg):
                after(dve, s_logc, tg, -(G - 1))
                hold(dve)
                for g in range(G):
                    mm = dve.max(top[:, g, :], logits[:, g, :])
                mm.then_inc(s_max8, G)

            def pick_numbers(tg):
                after(dve, s_max8, tg, -(G - 1))
                hold(dve)
                for g in range(G):
                    mm = dve.max_index(top_i[:, g, :], top[:, g, :], logits[:, g, :])
                mm.then_inc(s_idx, G)
                after(dve, s_tope, tg, 1)
                dve.tensor_tensor(top_d[:], top[:], top[:, :, 0:1].to_broadcast([P, G, E]), ALU.subtract).then_inc(s_topd, G)

            def as_float(tg):
                after(dve, s_idx, tg, -(G - 1))
                dve.tensor_copy(top_if[:], top_i[:, :, 0:2]).then_inc(s_idxf, G)

            def mark_chosen(tg):
                after(dve, s_idxf, tg, -(G - 1))
                dve.tensor_tensor(chosen[:], iota8.unsqueeze(1).unsqueeze(1).to_broadcast([P, G, 2, E]),
                                  top_if[:].unsqueeze(3).to_broadcast([P, G, 2, E]), ALU.is_equal).then_inc(s_chosen, G)

            def mark_members(tg):
                after(dve, s_chosen, tg, -(G - 1))
                after(dve, s_pos, tg, 1)
                dve.tensor_tensor(members[:], chosen[:, :, 0, :], chosen[:, :, 1, :], ALU.add).then_inc(s_members, G)

            def sum_members(tg):
                after(dve, s_members, tg, -(G - 1))
                dve.wait_ge(s_counted, tg + G)
                dve.reduce_sum(group_sum[:], members[:].rearrange("p g e -> p e g"), AX).then_inc(s_gsum, G)

            def place_rows(tg):
                after(dve, s_pos, tg, -(G - 1))
                dve.wait_ge(s_counted, tg + G)
                after(dve, s_gsum, tg, -(G - 1))
                dve.tensor_tensor(place[:].rearrange("p g e -> p (g e)"), ps_pos, region_base.unsqueeze(1).to_broadcast([P, G, E]), ALU.add).then_inc(s_place, G)
                dve.tensor_tensor(counted[:], counted[:], group_sum[:], ALU.add).then_inc(s_counted, G)

            def keep_chosen(tg):
                after(dve, s_place, tg, -(G - 1))
                dve.tensor_tensor(place2[:], chosen[:], place[:].unsqueeze(2).to_broadcast([P, G, 2, E]), ALU.mult).then_inc(s_place2, G)

            def slots(tg):
                after(dve, s_place2, tg, -(G - 1))
                after(dve, s_slotu, tg, 1)
                dve.reduce_sum(slot_f[:], place2[:], AX).then_inc(s_slotf, G)

            def gate_sums(tg):
                after(dve, s_tope, tg, -(G - 1))
                dve.reduce_sum(zsum[:], top_e[:], AX)
                dve.reduce_sum(two[:], top_e[:, :, 0:2], AX).then_inc(s_z, G)

            def gate_divisor(tg):
                after(dve, s_z, tg, -(G - 1))
                dve.scalar_tensor_tensor(out=gden[:], in0=zsum[:], scalar=1e-9, in1=two[:], op0=ALU.mult, op1=ALU.add).then_inc(s_gden, G)

            def gate_reciprocal(tg):
                after(dve, s_gden, tg, -(G - 1))
                dve.reciprocal(grec[:], gden[:]).then_inc(s_grec, G)

            def gate_values(tg):
                after(dve, s_grec, tg, -(G - 1))
                after(dve, s_meta, tg, 1)
                dve.tensor_tensor(gates[:], top_e[:, :, 0:2], grec[:].unsqueeze(2).to_broadcast([P, G, 2]), ALU.mult).then_inc(s_gates, G)

            def step(b, j, ok):
                s = b + j
                new, ln2, route, send = b + G, b - 2 * G, b - 3 * G, b - 4 * G
                t, par = s - LAG_PV, (j - LAG_PV) % 2
                if ok(t):
                    after(dve, s_pv, t, 0)
                    o = ps_pv.rearrange("p (a d) -> p a d", d=18)
                    dve.reciprocal(rden[:, par, :].rearrange("p (a d) -> p a d", d=2), o[:, :, 16:18]).then_inc(s_rden, 1)
                if j == 3 and ok(route):
                    as_float(route)
                if j == 0 and ok(send):
                    place_rows(send)
                if ok(t):
                    after(dve, s_rden, t, 0)
                    after(dve, s_ot, t, 2)
                    dve.tensor_tensor(att[:, par, :].rearrange("p (a h d) -> p a h d", h=2, d=HD),
                                      o[:, :, 0:16].rearrange("p a (h d) -> p a h d", d=HD),
                                      rden[:, par, :].rearrange("p (a h) -> p a h", h=2).unsqueeze(3).to_broadcast([P, 4, 2, HD]),
                                      ALU.mult).then_inc(s_att, 1)
                t, par = s - LAG_ROPE, (j - LAG_ROPE) % 2
                if ok(t):
                    after(dve, s_qkv, t, 0)
                    after(dve, s_qkbd, t, 1)
                    dve.tensor_tensor(rope[:].rearrange("p r a d -> p (r a d)"), ps_qkv[par][:, 0:2 * P], cos_sin, ALU.mult).then_inc(s_ropem, 1)
                if j == 3 and ok(route):
                    mark_chosen(route)
                if j == 0 and ok(send):
                    keep_chosen(send)
                if j == 1 and ok(new):
                    ln1_total(new)
                if ok(t):
                    after(dve, s_ropem, t, 0)
                    after(dve, s_turn, t, 2)
                    for w in range(2):
                        own = slice(w * N, (w + 1) * N)
                        mm = dve.tensor_tensor(qk_bd[own, par, :, w, :], rope[own, 0, :, :], rope[own, 1, :, :], ALU.add)
                    mm.then_inc(s_qkbd, 1)
                if j == 3 and ok(route):
                    mark_members(route)
                if j == 0 and ok(send):
                    slots(send)
                if j == 1 and ok(new):
                    ln1_average(new)
                t, par = s - LAG_MAX, (j - LAG_MAX) % 2
                if ok(t):
                    after(dve, s_score, t, 0)
                    sc = ps_score[par][:, :].rearrange("p (h k) -> p h k", k=N)
                    dve.reduce_max(smax[:, par, :], sc, AX).then_inc(s_max, 1)
                if j == 3 and ok(route):
                    sum_members(route)
                if j == 0 and ok(send):
                    gate_sums(send)
                if j == 2 and ok(new):
                    ln1_squares(new)
                t, par = s - LAG_MAX, (j - LAG_MAX) % 2
                if ok(t):
                    after(dve, s_max, t, 0)
                    after(dve, s_pt, t, 2)
                    dve.tensor_tensor(probs[:, par, :, :], sc, smax[:, par, :].unsqueeze(2).to_broadcast([P, HEADS, N]), ALU.subtract).then_inc(s_sub, 1)
                t, par = s - LAG_PROJ, (j - LAG_PROJ) % 2
                if ok(t):
                    after(dve, s_proj, t, 0)
                    dve.tensor_tensor(res_all[:, t, :], ps_proj, res_all[:, t, :], ALU.add).then_inc(s_t, 1)
                if j == 0 and ok(send):
                    gate_divisor(send)
                if j == 0 and ok(route):
                    ln2_squares(route)
                if j == 2 and ok(new):
                    ln1_variance(new)
                t, par = s - LAG_KBD, (j - LAG_KBD) % 2
                if ok(t):
                    after(dve, s_qktc, t, 0)
                    after(dve, s_score, t, 2)
                    dve.tensor_tensor(k_bd[:, par, :, :], qkt[:, par, P:P + N].unsqueeze(1).to_broadcast([P, HEADS, N]),
                                      head_mask.unsqueeze(2).to_broadcast([P, HEADS, N]), ALU.mult).then_inc(s_kbd, 1)
                if j == 0 and ok(send):
                    gate_reciprocal(send)
                if j == 0 and ok(route):
                    ln2_variance(route)
                if j == 0 and ok(send):
                    gate_values(send)
                if j == 2 and ok(route):
                    pick(route)
                if j == 2 and ok(route):
                    pick_numbers(route)
                if j == 3 and ok(ln2):
                    ln2_total(ln2)
                if j == 3 and ok(ln2):
                    ln2_average(ln2)

            dve.wait_ge(x_in, 16)
            ln1_total(0)
            ln1_average(0)
            dve.wait_ge(c_in, 16)
            dve.wait_ge(w_in, 16)
            for w in range(2):
                for g in range(G):
                    mm = dve.tensor_copy(v_bd[:, g, w, :, 16:18], v_mask.unsqueeze(1).to_broadcast([P, 4, 2]))
            mm.then_inc(init_s, 1)
            dve.tensor_copy(wext[:, 0:P], wqkv_sb[:, 0:P]).then_inc(wext_s, 1)
            dve.tensor_copy(wext[:, 2 * P:2 * P + C], wqkv_sb[:, P:QKV]).then_inc(wext_s, 1)
            src = wqkv_sb[:, 0:P].rearrange("p (g h d) -> p g h d", h=2, d=2)
            dst = wext[:, P:2 * P].rearrange("p (g h d) -> p g h d", h=2, d=2)
            dve.tensor_copy(dst[:, :, 0, :], src[:, :, 1, :])
            dve.tensor_copy(dst[:, :, 1, :], src[:, :, 0, :]).then_inc(wext_s, 1)
            ln1_squares(0)
            ln1_variance(0)
            dve.wait_ge(init_s, 4)

            def body(b, ok, masked):
                if isinstance(b, int) and b == FIRST_TILES - 2 * G:
                    dve.wait_ge(rest_in, 32)
                if isinstance(b, int) and b == LAG_PROJ:
                    dve.wait_ge(res_in, 16)
                for j in range(G):
                    step(b, j, ok)
                    wt = split_group(b, masked)
                    if j == 2 and wt is not None:
                        dve.wait_ge(s_whi, wt + G)
                        dve.tensor_tensor(wraw[:], wraw[:], wparts[:, 0, :], ALU.subtract).then_inc(s_wrest, G)
                    if j == 3 and wt is not None:
                        dve.wait_ge(s_wmid, wt + G)
                        dve.tensor_tensor(wparts[:, 2, :], wraw[:], wparts[:, 1, :], ALU.subtract).then_inc(s_wlo, G)
            groups(dve, body)

            dve.wait_ge(s_cnt, 1)
            dve.tensor_copy(cnt_f[:], ps_cnt).then_inc(s_tstep, 1)
            dve.wait_ge(s_tstep, 1)
            dve.tensor_scalar(til_f[:], cnt_f[:], float(SLOTS - 1), None, ALU.add).then_inc(s_tstep, 1)
            dve.tensor_tensor(padrow_f[:], cnt_f[:], region_base, ALU.add).then_inc(s_tstep, 1)
            dve.wait_ge(s_tstep, 3)
            dve.tensor_copy(til_i[:], til_f[:]).then_inc(s_tstep, 1)
            dve.tensor_copy(padrow_i[:], padrow_f[:]).then_inc(s_tstep, 1)
            dve.wait_ge(s_tstep, 5)
            dve.tensor_scalar(til_s[:], til_i[:], P.bit_length() - 1, None, ALU.arith_shift_right).then_inc(s_tstep, 1)
            dve.wait_ge(s_tstep, 6)
            dve.tensor_copy(til_f[:], til_s[:]).then_inc(s_tstep, 1)
            dve.wait_ge(s_tstep, 7)
            dve.tensor_scalar(til_m[:], til_f[:], float(THIRD), None, ALU.mult).then_inc(s_tstep, 1)
            dve.wait_ge(s_tstep, 8)
            dve.tensor_copy(til_i[:], til_m[:]).then_inc(s_tstep, 1)
            dve.wait_ge(s_tstep, 9)
            dve.tensor_scalar(til_s[:], til_i[:], THIRD_SHIFT, None, ALU.arith_shift_right).then_inc(s_tstep, 1)
            dve.wait_ge(s_tstep, 10)
            dve.tensor_copy(til_f[:], til_s[:]).then_inc(s_tstep, 1)
            dve.wait_ge(s_tstep, 11)
            dve.tensor_scalar(til_m[:], til_f[:], 1.0, None, ALU.max).then_inc(s_tstep, 1)
            dve.wait_ge(s_tstep, 12)
            dve.tensor_tensor_scan(ends_f[:], til_m[:], zero8[:], 0.0, ALU.add, ALU.add).then_inc(s_tstep, 1)
            dve.wait_ge(s_tstep, 13)
            dve.tensor_copy(ends_i[:], ends_f[:]).then_inc(s_tile, 1)
            dve.engine_nop().then_inc(s_hid, 2)
            dve.engine_nop().then_inc(s_x2, 1)
            dve.engine_nop().then_inc(s_yb, 1)
            dve.engine_nop().then_inc(s_yout, 1)
            dve.engine_nop().then_inc(s_nextmeta, 1)

            def copy_rows(n):
                dve.wait_ge(s_x2, n + 2)
                dve.tensor_copy(xs[:, 1, :], ps_x[1][:, 0:SLOTS]).then_inc(s_xs[1], 1)

            def tail(k):
                dve.wait_ge(s_yt, k + 1)
                dve.wait_ge(s_tailmeta, k + 1)
                dve.wait_ge(s_yout, k + 1)
                y4 = ps_yt[:, :].rearrange("p (c h d) -> p c h d", h=2, d=C)
                gate = meta[:].bitcast(F32)[:, :, 0:1].to_broadcast([P, SUB, C])
                dve.tensor_tensor(y_a[:], y4[:, :, 0, :], gate, ALU.mult)
                dve.tensor_tensor(y_b[:], y4[:, :, 1, :], gate, ALU.mult).then_inc(s_yb, 1)

            copy_rows(0)
            start = 0
            for e in range(E):
                end = dve.value_load(ends_i[0:1, e:e + 1], min_val=e + 1, max_val=MAX_TILES)
                with dve.Fori(start, end) as n:
                    for c in range(CHUNKS):
                        q = n * CHUNKS + c
                        dve.wait_ge(s_silu, q + 1)
                        if c < FULL:
                            dve.wait_ge(s_g, n * FULL + (c + 1))
                        dve.wait_ge(s_yc, q + 1)
                        if c < FULL:
                            dve.tensor_tensor(hid[:, c % 3, :], gate_h[:, c % 2, :], ps_g[c % 2][:, :], ALU.mult).then_inc(s_hid, 1)
                        else:
                            dve.tensor_tensor(hid[0:C, c % 3, :], gate_h[0:C, c % 2, :], ps_h[c % 2][C:2 * C, :], ALU.mult).then_inc(s_hid, 1)
                        if c == 0:
                            tail(n)
                    copy_rows(n + 1)
                start = end
            tail(start)

        @block.gpsimd
        def _(pool):
            pool.memset(minus_half[:], -0.5).then_inc(s_half, 1)
            pool.wait_ge(x_in, 16)
            pool.wait_ge(s_half, 1)

            def center(x, mean, c, sq, s_mean, s_c, s_sq, s_var, s_norm, tg):
                after(pool, s_mean, tg, -(G - 1))
                after(pool, s_norm, tg, 1)
                pool.tensor_tensor(c[:], x, mean[:].unsqueeze(2).to_broadcast([P, G, C]), ALU.subtract).then_inc(s_c, G)
                after(pool, s_c, tg, -(G - 1))
                after(pool, s_var, tg, 1)
                pool.tensor_tensor(sq[:], c[:], c[:], ALU.mult).then_inc(s_sq, G)

            def scale1(tg, half):
                a = half * 2
                if half == 0:
                    after(pool, s1vare, tg, -(G - 1))
                    pool.tensor_tensor(ln1_rstd[:], ln1_vare[:], minus_half[:], ALU.pow).then_inc(s1rstd, G)
                after(pool, s1rstd, tg, -(G - 1))
                after(pool, s_xt, tg - G + a + 1, 0)
                pool.tensor_tensor(xn[:, a:a + 2, :], ln1_c[:, a:a + 2, :], ln1_rstd[:, a:a + 2].unsqueeze(2).to_broadcast([P, 2, C]), ALU.mult).then_inc(s1xn, 2)

            def scatter(tg, picks):
                for i in picks:
                    pool.indirect_dma_start(rows_dram, bass.IndirectOffsetOnAxis(ap=slot_u[:, i // 2, i % 2:i % 2 + 1], axis=0),
                                            rows[:, i // 2, i % 2, :], None).then_inc(s_scat, 16)

            def fill_meta(tg):
                after(pool, s_scat, tg, 1, 32)
                after(pool, s_gates, tg, -(G - 1))
                after(pool, s_slotf, tg, -(G - 1))
                hold(pool)
                m = rows[:, :, :, PARTS:ROW]
                pool.tensor_copy(m.bitcast(F32)[:, :, :, 0], gates[:])
                pool.tensor_copy(m[:, :, :, 1], tok_sb[:, tiles_of(tg)].unsqueeze(2).to_broadcast([P, G, 2])).then_inc(s_meta, G)
                pool.tensor_copy(slot_u[:], slot_f[:]).then_inc(s_slotu, G)
                after(pool, s_slotu, tg, -(G - 1))
                after(pool, s_meta, tg, -(G - 1))
                after(pool, s_rows, tg, -(G - 1))
                hold(pool)

            center(x_all[:, 0:G, :], ln1_mean, ln1_c, ln1_sq, s1mean, s1c, s1sq, s1var, s1xn, 0)
            scale1(0, 0)
            scale1(0, 1)

            def body(b, ok, masked):
                if isinstance(b, int) and b == FIRST_TILES - 2 * G:
                    pool.wait_ge(rest_in, 32)
                if isinstance(b, int) and b == 4 * G:
                    pool.wait_ge(cb_in, 48)
                for j in range(G):
                    tg = b - 4 * G
                    if j == 1 and ok(tg):
                        fill_meta(tg)
                    if j >= 1 and ok(tg):
                        scatter(tg, ((), (0, 1), (2, 3, 4), (5, 6, 7))[j])
                    tg = b - 3 * G
                    if j == 0 and ok(tg):
                        after(pool, s2vare, tg, -(G - 1))
                        pool.tensor_tensor(ln2_rstd[:], ln2_vare[:], minus_half[:], ALU.pow).then_inc(s2rstd, G)
                        after(pool, s2rstd, tg, -(G - 1))
                        after(pool, s_x2t, tg, 1)
                        after(pool, s_rest, tg, 1)
                        pool.tensor_tensor(xn2[:], ln2_c[:], ln2_rstd[:].unsqueeze(2).to_broadcast([P, G, C]), ALU.mult).then_inc(s2xn, G)
                    if j == 2 and ok(tg):
                        after(pool, s_hi, tg, -(G - 1))
                        after(pool, s_lo, tg, 1)
                        pool.tensor_tensor(split_r[:], xn2[:], parts[:, :, 1, :], ALU.subtract).then_inc(s_rest, G)
                    if j == 3 and ok(tg):
                        after(pool, s_mid, tg, -(G - 1))
                        pool.tensor_tensor(parts[:, :, 2, :], split_r[:], parts[:, :, 0, :], ALU.subtract).then_inc(s_lo, G)
                    tg = b + G
                    if j == 1 and ok(tg):
                        center(x_all[:, tiles_of(tg), :], ln1_mean, ln1_c, ln1_sq, s1mean, s1c, s1sq, s1var, s1xn, tg)
                    if j == 2 and ok(tg):
                        scale1(tg, 0)
                    if j == 3 and ok(tg):
                        scale1(tg, 1)
                    tg = b - 2 * G
                    if j == 3 and ok(tg):
                        center(res_all[:, tiles_of(tg), :], ln2_mean, ln2_c, ln2_sq, s2mean, s2c, s2sq, s2var, s2xn, tg)
            groups(pool, body)
            pool.engine_nop().then_inc(s_yc, 3)

            def add_rows(k):
                pool.wait_ge(s_yb, k + 2)
                pool.tensor_tensor(y_out[:], y_a[:], y_b[:], ALU.add).then_inc(s_yout, 1)
                pool.wait_ge(s_yout, k + 2)
                hold(pool)
                for c in range(SUB):
                    pool.indirect_dma_start(out, bass.IndirectOffsetOnAxis(ap=meta[:, c, 1:2], axis=0),
                                            y_out[:, c, :], None, compute_op=ALU.add).then_inc(s_added, 16)
                pool.wait_ge(s_added, (k + 1) * (16 * SUB))
                hold(pool)

            def keep_meta(n):
                pool.wait_ge(s_xin, (n + 1) * 16)
                pool.wait_ge(s_tailmeta, n + 1)
                hold(pool)
                pool.tensor_copy(meta_next[:], xin[:, :, PARTS:ROW]).then_inc(s_nextmeta, 1)

            pool.tensor_copy(meta[:], pad_sb[:, :, PARTS:ROW]).then_inc(s_tailmeta, 1)
            pool.wait_ge(s_tout, 16 * GROUPS)
            pool.wait_ge(s_dummy, 16)
            keep_meta(0)
            pool.wait_ge(s_tile, 2)
            start = 0
            for e in range(E):
                end = pool.value_load(ends_i[0:1, e:e + 1], min_val=e + 1, max_val=MAX_TILES)
                with pool.Fori(start, end) as n:
                    add_rows(n)
                    pool.wait_ge(s_nextmeta, n + 2)
                    hold(pool)
                    pool.tensor_copy(meta[:], meta_next[:]).then_inc(s_tailmeta, 1)
                    keep_meta(n + 1)
                start = end
            add_rows(start)


def window_order():
    n_side = SIDE // (WIN * DIL)
    wins, masked = [], []
    for img in range(BATCH):
        for w in range(PER_IMAGE):
            (masked if w >= PER_IMAGE - MASKED_PER_IMAGE else wins).append((img, w))
    src, dst = [], []
    for img, w in wins + masked:
        block, d = divmod(w, DIL * DIL)
        bh, bw = divmod(block, n_side)
        dh, dw = divmod(d, DIL)
        base = (img * PER_IMAGE + w) * N
        for n in range(N):
            i, j = divmod(n, WIN)
            row = (bh * WIN * DIL + i * DIL + dh + SHIFT) % SIDE
            col = (bw * WIN * DIL + j * DIL + dw + SHIFT) % SIDE
            src.append(base + n)
            dst.append((img * SIDE + row) * SIDE + col)
    return np.array(src), np.array(dst)


def constants():
    kf = np.zeros((P, K_COLS), np.float32)
    kf[:, K_IDENT:K_IDENT + P] = np.eye(P)
    half = HD // 4
    inv = (1.0 / 10000.0 ** (np.arange(half, dtype=np.float32) / half)).astype(np.float32)
    tok = np.arange(P) % N
    for ax, pos in enumerate((tok // WIN, tok % WIN)):
        ang = pos[:, None].astype(np.float32) * inv
        for hh in range(2):
            for d in range(half):
                for head in range(HEADS):
                    col = head * HD + ax * (HD // 2) + hh * half + d
                    for which, scale in enumerate((HD ** -0.5, 1.0)):
                        kf[:, K_COS + which * C + col] = np.cos(ang[:, d]) * scale
                        kf[:, K_SIN + which * C + col] = np.sin(ang[:, d]) * scale * (1, -1)[hh == 0]
    kf[np.arange(P), K_PAIR + np.arange(P) % N] = 1
    kf[np.arange(P), K_HEADMASK + (np.arange(P) % C) // HD] = 1
    kf[np.arange(P), K_VMASK + np.arange(P) // N] = 1
    kf[:, K_IOTA:K_IOTA + E] = np.arange(E)
    kf[:, K_BASE:K_BASE + E] = np.arange(E) * REGION
    kb = np.zeros((P, B_COLS), np.float32)
    kb[:, B_IDENT:B_IDENT + P] = np.eye(P)
    kb[:, B_TRI:B_TRI + P] = np.arange(P)[:, None] < np.arange(P)[None, :]
    kb[:, B_ONES:B_ONES + P] = 1
    region = np.digitize(np.arange(N) // WIN, (WIN // 2, WIN // 2 + SHIFT // DIL))
    kb[:, B_MASK:B_MASK + N] = np.where(region[tok][:, None] != region[None, :], BIG, 0)
    tok_id = (np.arange(TILES)[None, :] * P + np.arange(P)[:, None]).astype(np.uint32)
    pad = np.zeros((P, SUB, ROW), np.uint32)
    pad[:, :, ROW - 1] = TOKENS + np.arange(SUB)[None, :] * P + np.arange(P)[:, None]
    return kf, (kb.view(np.uint32) >> 16).astype(np.uint16), tok_id, pad


def kernel(x, L0_conv_W_qkv, L0_conv_b_qkv, L0_conv_W_proj, L0_conv_b_proj, L0_ffn_router_w, L0_ffn_w1, L0_ffn_w2, L0_ffn_w3):
    import concourse.bacc as bacc
    from concourse.bass_utils import run_bass_kernel_spmd

    x = np.asarray(x)
    src, dst = window_order()
    flat = x.reshape(TOKENS, C)
    w1, w2, w3 = (np.asarray(a) for a in (L0_ffn_w1, L0_ffn_w2, L0_ffn_w3))
    w13 = np.zeros((E, C, 2 * WHALF), np.float32)
    for c in range(FULL):
        w13[:, :, 2 * c * P:(2 * c + 1) * P] = w1[:, c * P:(c + 1) * P, :].transpose(0, 2, 1)
        w13[:, :, (2 * c + 1) * P:(2 * c + 2) * P] = w3[:, c * P:(c + 1) * P, :].transpose(0, 2, 1)
    w13[:, :, 2 * FULL * P:2 * FULL * P + REST] = w1[:, FULL * P:, :].transpose(0, 2, 1)
    w13[:, :, 2 * FULL * P + C:2 * FULL * P + C + REST] = w3[:, FULL * P:, :].transpose(0, 2, 1)
    w2t = np.zeros((P, E, CHUNKS, C), np.float32)
    for c in range(CHUNKS):
        k = min(P, H - c * P)
        w2t[0:k, :, c, :] = w2[:, :, c * P:c * P + k].transpose(2, 0, 1)
    router = np.zeros((P, 2 * E), np.float32)
    router[0:C, 0:E] = np.asarray(L0_ffn_router_w).T
    router[C:2 * C, E:2 * E] = np.asarray(L0_ffn_router_w).T
    kf, kb, tok_id, pad = constants()
    arrays = {
        "x_win": flat[src].reshape(TILES, P, C).transpose(1, 0, 2).copy(), "x_res": flat[dst].reshape(TILES, P, C).transpose(1, 0, 2).copy(),
        "w_qkv": np.concatenate([np.asarray(L0_conv_W_qkv), np.asarray(L0_conv_b_qkv)[None, :]], 0),
        "w_proj": np.concatenate([np.asarray(L0_conv_W_proj), np.asarray(L0_conv_b_proj)[None, :]], 0),
        "router": router, "w13": w13.reshape(E, C, 2, WHALF).transpose(0, 2, 1, 3).reshape(E, P, WHALF), "w2": w2t, "kf": kf, "kb": kb, "tok_id": tok_id, "pad_rows": pad,
    }
    nc = bacc.Bacc("TRN2", target_bir_lowering=False, num_devices=1)
    args = {n: nc.dram_tensor(n, a.shape, mybir.dt.from_np(a.dtype), kind="ExternalInput").ap() for n, a in arrays.items()}
    out = nc.dram_tensor("out", (TOKENS + SLOTS, C), F32, kind="ExternalOutput").ap()
    build(nc, out=out, **args)
    r = run_bass_kernel_spmd(nc, [arrays], core_ids=[0])
    rows = np.asarray(r.results[0]["out"])
    y = np.empty((TOKENS, C), np.float32)
    y[dst] = rows[0:TOKENS]
    return y.reshape(x.shape)
```
